# Optimizing a Trainium2 kernel written in Bass

```python
import numpy as np
import jax
import jax.numpy as jnp

def _softmax(x, axis=-1):
    return jax.nn.softmax(x, axis=axis)

def _gelu(x):
    return jax.nn.gelu(x, approximate=True)

def _silu(x):
    return jax.nn.silu(x)

def _sigmoid(x):
    return jax.nn.sigmoid(x)

def _layernorm(x, axis=-1, eps=1e-05):
    m = jnp.mean(x, axis=axis, keepdims=True)
    v = jnp.var(x, axis=axis, keepdims=True)
    return (x - m) / jnp.sqrt(v + eps)

def _scatter_add(tgt, idx, src, axis=0):
    return tgt.at[idx].add(src)

def _segment_sum(src, seg, n):
    return jax.ops.segment_sum(src, seg, n)
kernel_name = 'mk_hybrid_d1_jaxref_r8_8e816c'

def setup_inputs(seed: int=0):
    np.random.seed(seed)
    _w = jnp.asarray

    def _L0_attn_a_setup():
        import jax, jax.numpy as jnp
        import numpy as np
        D_MODEL = 128
        N_HEADS = 16
        HEAD_DIM = D_MODEL // N_HEADS
        EPS_ATTN = 1e-06
        EPS_LN = 1e-05

        def layer_norm(x, gamma, beta):
            mu = jnp.mean(x, axis=-1, keepdims=True)
            var = jnp.var(x, axis=-1, keepdims=True)
            return (x - mu) * jax.lax.rsqrt(var + EPS_LN) * gamma + beta

        def linear_attention(x, Wq, bq, Wk, bk, Wv, bv, Wo, bo):
            N, L, _ = x.shape
            H, Dh = (N_HEADS, HEAD_DIM)
            Q = (x @ Wq + bq).reshape(N, L, H, Dh)
            K = (x @ Wk + bk).reshape(N, L, H, Dh)
            V = (x @ Wv + bv).reshape(N, L, H, Dh)
            Q = jax.nn.elu(Q) + 1.0
            K = jax.nn.elu(K) + 1.0
            KV = jnp.einsum('nshd,nshm->nhmd', K, V)
            Ksum = K.sum(axis=1)
            Z = 1.0 / (jnp.einsum('nlhd,nhd->nlh', Q, Ksum) + EPS_ATTN)
            out = jnp.einsum('nlhd,nhmd,nlh->nlhm', Q, KV, Z)
            out = out.reshape(N, L, H * Dh)
            return out @ Wo + bo
        key = jax.random.key(seed)
        ks = jax.random.split(key, 16)
        s = 1.0 / np.sqrt(D_MODEL)
        inp = {'x': jax.random.normal(ks[0], (4, 512, D_MODEL), dtype=jnp.float32), 'Wq': jax.random.normal(ks[1], (D_MODEL, D_MODEL), dtype=jnp.float32) * s, 'bq': jnp.zeros((D_MODEL,), jnp.float32), 'Wk': jax.random.normal(ks[2], (D_MODEL, D_MODEL), dtype=jnp.float32) * s, 'bk': jnp.zeros((D_MODEL,), jnp.float32), 'Wv': jax.random.normal(ks[3], (D_MODEL, D_MODEL), dtype=jnp.float32) * s, 'bv': jnp.zeros((D_MODEL,), jnp.float32), 'Wo': jax.random.normal(ks[4], (D_MODEL, D_MODEL), dtype=jnp.float32) * s, 'bo': jnp.zeros((D_MODEL,), jnp.float32), 'W1': jax.random.normal(ks[5], (D_MODEL, 4 * D_MODEL), dtype=jnp.float32) * s, 'b1': jnp.zeros((4 * D_MODEL,), jnp.float32), 'W2': jax.random.normal(ks[6], (4 * D_MODEL, D_MODEL), dtype=jnp.float32) * (0.5 * s), 'b2': jnp.zeros((D_MODEL,), jnp.float32), 'g1': jnp.ones((D_MODEL,), jnp.float32), 'beta1': jnp.zeros((D_MODEL,), jnp.float32), 'g2': jnp.ones((D_MODEL,), jnp.float32), 'beta2': jnp.zeros((D_MODEL,), jnp.float32)}
        return inp
    _L0_attn_a_in = _L0_attn_a_setup()

    def _L0_attn_b_setup():
        import math
        import jax, jax.numpy as jnp
        import numpy as np
        B, L, D_MODEL = (2, 256, 128)
        N_HEAD, HEAD_DIM = (16, 64)
        ATT_SCALE = 1.0
        key = jax.random.key(seed)
        ks = jax.random.split(key, 6)
        HD = N_HEAD * HEAD_DIM

        def xavier(k, fan_in, fan_out):
            lim = math.sqrt(6.0 / (fan_in + fan_out))
            return jax.random.uniform(k, (fan_in, fan_out), jnp.float32, -lim, lim)
        return {'x': jax.random.normal(ks[0], (B, L, D_MODEL), jnp.float32), 'Wq': xavier(ks[1], D_MODEL, HD), 'bq': jnp.zeros((HD,), jnp.float32), 'Wk': xavier(ks[2], D_MODEL, HD), 'bk': jnp.zeros((HD,), jnp.float32), 'Wv': xavier(ks[3], D_MODEL, HD), 'bv': jnp.zeros((HD,), jnp.float32), 'Wo': xavier(ks[4], HD, D_MODEL), 'bo': jax.random.uniform(ks[5], (D_MODEL,), jnp.float32, -1.0 / math.sqrt(HD), 1.0 / math.sqrt(HD))}
    _L0_attn_b_in = _L0_attn_b_setup()

    def _L0_ffn_setup():
        import jax, jax.numpy as jnp
        import numpy as np
        D = 128
        H = 4
        DF = 512
        E = 8
        EPS = 1e-05

        def _layer_norm(x, g, b):
            mu = jnp.mean(x, axis=-1, keepdims=True)
            var = jnp.mean(jnp.square(x - mu), axis=-1, keepdims=True)
            return (x - mu) * jax.lax.rsqrt(var + EPS) * g + b

        def _mha(x, Wqkv, bqkv, Wo, bo):
            S, B, _ = x.shape
            hd = D // H
            qkv = x @ Wqkv.T + bqkv
            q, k, v = jnp.split(qkv, 3, axis=-1)
            to_heads = lambda t: t.reshape(S, B, H, hd).transpose(1, 2, 0, 3)
            q, k, v = (to_heads(q), to_heads(k), to_heads(v))
            scores = jnp.einsum('bhqd,bhkd->bhqk', q, k) * (1.0 / np.sqrt(hd))
            att = jax.nn.softmax(scores, axis=-1)
            o = jnp.einsum('bhqk,bhkd->bhqd', att, v)
            o = o.transpose(2, 0, 1, 3).reshape(S, B, D)
            return o @ Wo.T + bo

        def _moe(x, Wg, W1, b1, W2, b2):
            S, B, _ = x.shape
            xf = x.reshape(S * B, D)
            logits = xf @ Wg.T
            idx = jnp.argmax(logits, axis=-1)
            out = jnp.zeros_like(xf)
            for e in range(E):
                m = (idx == e)[:, None].astype(xf.dtype)
                h = jax.nn.relu(xf @ W1[e] + b1[e])
                out = out + m * (h @ W2[e] + b2[e])
            return out.reshape(S, B, D)
        key = jax.random.key(seed)
        ks = jax.random.split(key, 16)
        S, B = (64, 8)
        s = lambda k, shape, fan: jax.random.normal(k, shape, jnp.float32) * (1.0 / np.sqrt(fan))
        return {'x': jax.random.normal(ks[0], (S, B, D), jnp.float32), 'Wqkv': s(ks[1], (3 * D, D), D), 'bqkv': jnp.zeros((3 * D,), jnp.float32), 'Wo': s(ks[2], (D, D), D), 'bo': jnp.zeros((D,), jnp.float32), 'g1': jnp.ones((D,), jnp.float32), 'be1': jnp.zeros((D,), jnp.float32), 'g2': jnp.ones((D,), jnp.float32), 'be2': jnp.zeros((D,), jnp.float32), 'Wg': s(ks[3], (E, D), D), 'W1': s(ks[4], (E, D, DF), D), 'b1': jnp.zeros((E, DF), jnp.float32), 'W2': s(ks[5], (E, DF, D), DF), 'b2': jnp.zeros((E, D), jnp.float32)}
    _L0_ffn_in = _L0_ffn_setup()
    _d = {'L0_attn_a_x': _L0_attn_a_in['x'], 'L0_attn_a_Wq': _L0_attn_a_in['Wq'], 'L0_attn_a_bq': _L0_attn_a_in['bq'], 'L0_attn_a_Wk': _L0_attn_a_in['Wk'], 'L0_attn_a_bk': _L0_attn_a_in['bk'], 'L0_attn_a_Wv': _L0_attn_a_in['Wv'], 'L0_attn_a_bv': _L0_attn_a_in['bv'], 'L0_attn_a_Wo': _L0_attn_a_in['Wo'], 'L0_attn_a_bo': _L0_attn_a_in['bo'], 'L0_attn_a_W1': _L0_attn_a_in['W1'], 'L0_attn_a_b1': _L0_attn_a_in['b1'], 'L0_attn_a_W2': _L0_attn_a_in['W2'], 'L0_attn_a_b2': _L0_attn_a_in['b2'], 'L0_attn_a_g1': _L0_attn_a_in['g1'], 'L0_attn_a_beta1': _L0_attn_a_in['beta1'], 'L0_attn_a_g2': _L0_attn_a_in['g2'], 'L0_attn_a_beta2': _L0_attn_a_in['beta2'], 'L0_attn_b_Wq': _L0_attn_b_in['Wq'], 'L0_attn_b_bq': _L0_attn_b_in['bq'], 'L0_attn_b_Wk': _L0_attn_b_in['Wk'], 'L0_attn_b_bk': _L0_attn_b_in['bk'], 'L0_attn_b_Wv': _L0_attn_b_in['Wv'], 'L0_attn_b_bv': _L0_attn_b_in['bv'], 'L0_attn_b_Wo': _L0_attn_b_in['Wo'], 'L0_attn_b_bo': _L0_attn_b_in['bo'], 'L0_ffn_Wqkv': _L0_ffn_in['Wqkv'], 'L0_ffn_bqkv': _L0_ffn_in['bqkv'], 'L0_ffn_Wo': _L0_ffn_in['Wo'], 'L0_ffn_bo': _L0_ffn_in['bo'], 'L0_ffn_g1': _L0_ffn_in['g1'], 'L0_ffn_be1': _L0_ffn_in['be1'], 'L0_ffn_g2': _L0_ffn_in['g2'], 'L0_ffn_be2': _L0_ffn_in['be2'], 'L0_ffn_Wg': _L0_ffn_in['Wg'], 'L0_ffn_W1': _L0_ffn_in['W1'], 'L0_ffn_b1': _L0_ffn_in['b1'], 'L0_ffn_W2': _L0_ffn_in['W2'], 'L0_ffn_b2': _L0_ffn_in['b2']}
    _x0 = _d['L0_attn_a_x']
    _d['L0_attn_a_x'] = jax.random.normal(jax.random.fold_in(jax.random.key(seed), 1), (16, 256, 128), dtype=_x0.dtype)
    del _x0
    return _d

def reference(L0_attn_a_x, L0_attn_a_Wq, L0_attn_a_bq, L0_attn_a_Wk, L0_attn_a_bk, L0_attn_a_Wv, L0_attn_a_bv, L0_attn_a_Wo, L0_attn_a_bo, L0_attn_a_W1, L0_attn_a_b1, L0_attn_a_W2, L0_attn_a_b2, L0_attn_a_g1, L0_attn_a_beta1, L0_attn_a_g2, L0_attn_a_beta2, L0_attn_b_Wq, L0_attn_b_bq, L0_attn_b_Wk, L0_attn_b_bk, L0_attn_b_Wv, L0_attn_b_bv, L0_attn_b_Wo, L0_attn_b_bo, L0_ffn_Wqkv, L0_ffn_bqkv, L0_ffn_Wo, L0_ffn_bo, L0_ffn_g1, L0_ffn_be1, L0_ffn_g2, L0_ffn_be2, L0_ffn_Wg, L0_ffn_W1, L0_ffn_b1, L0_ffn_W2, L0_ffn_b2):

    def _L0_attn_a_ref(x, Wq, bq, Wk, bk, Wv, bv, Wo, bo, W1, b1, W2, b2, g1, beta1, g2, beta2):
        import jax, jax.numpy as jnp
        import numpy as np
        D_MODEL = 128
        N_HEADS = 16
        HEAD_DIM = D_MODEL // N_HEADS
        EPS_ATTN = 1e-06
        EPS_LN = 1e-05

        def layer_norm(x, gamma, beta):
            mu = jnp.mean(x, axis=-1, keepdims=True)
            var = jnp.var(x, axis=-1, keepdims=True)
            return (x - mu) * jax.lax.rsqrt(var + EPS_LN) * gamma + beta

        def linear_attention(x, Wq, bq, Wk, bk, Wv, bv, Wo, bo):
            N, L, _ = x.shape
            H, Dh = (N_HEADS, HEAD_DIM)
            Q = (x @ Wq + bq).reshape(N, L, H, Dh)
            K = (x @ Wk + bk).reshape(N, L, H, Dh)
            V = (x @ Wv + bv).reshape(N, L, H, Dh)
            Q = jax.nn.elu(Q) + 1.0
            K = jax.nn.elu(K) + 1.0
            KV = jnp.einsum('nshd,nshm->nhmd', K, V)
            Ksum = K.sum(axis=1)
            Z = 1.0 / (jnp.einsum('nlhd,nhd->nlh', Q, Ksum) + EPS_ATTN)
            out = jnp.einsum('nlhd,nhmd,nlh->nlhm', Q, KV, Z)
            out = out.reshape(N, L, H * Dh)
            return out @ Wo + bo
        x = x + linear_attention(x, Wq, bq, Wk, bk, Wv, bv, Wo, bo)
        x = layer_norm(x, g1, beta1)
        y = jax.nn.relu(x @ W1 + b1) @ W2 + b2
        return layer_norm(x + y, g2, beta2)

    def _L0_attn_b_ref(x, Wq, bq, Wk, bk, Wv, bv, Wo, bo):
        import math
        import jax, jax.numpy as jnp
        import numpy as np
        B, L, D_MODEL = (2, 256, 128)
        N_HEAD, HEAD_DIM = (16, 64)
        ATT_SCALE = 1.0
        b, l, _ = x.shape
        q = (x @ Wq + bq).reshape(b, l, N_HEAD, HEAD_DIM)
        k = (x @ Wk + bk).reshape(b, l, N_HEAD, HEAD_DIM)
        v = (x @ Wv + bv).reshape(b, l, N_HEAD, HEAD_DIM)
        scale = 1.0 / math.sqrt(HEAD_DIM ** ATT_SCALE)
        scores = jnp.einsum('blhd,bmhd->bhlm', q, k) * scale
        attn = jnp.einsum('bhlm,bmhd->blhd', scores, v)
        out = attn.reshape(b, l, N_HEAD * HEAD_DIM) @ Wo + bo
        return out

    def _L0_ffn_ref(x, Wqkv, bqkv, Wo, bo, g1, be1, g2, be2, Wg, W1, b1, W2, b2):
        import jax, jax.numpy as jnp
        import numpy as np
        D = 128
        H = 4
        DF = 512
        E = 8
        EPS = 1e-05

        def _layer_norm(x, g, b):
            mu = jnp.mean(x, axis=-1, keepdims=True)
            var = jnp.mean(jnp.square(x - mu), axis=-1, keepdims=True)
            return (x - mu) * jax.lax.rsqrt(var + EPS) * g + b

        def _mha(x, Wqkv, bqkv, Wo, bo):
            S, B, _ = x.shape
            hd = D // H
            qkv = x @ Wqkv.T + bqkv
            q, k, v = jnp.split(qkv, 3, axis=-1)
            to_heads = lambda t: t.reshape(S, B, H, hd).transpose(1, 2, 0, 3)
            q, k, v = (to_heads(q), to_heads(k), to_heads(v))
            scores = jnp.einsum('bhqd,bhkd->bhqk', q, k) * (1.0 / np.sqrt(hd))
            att = jax.nn.softmax(scores, axis=-1)
            o = jnp.einsum('bhqk,bhkd->bhqd', att, v)
            o = o.transpose(2, 0, 1, 3).reshape(S, B, D)
            return o @ Wo.T + bo

        def _moe(x, Wg, W1, b1, W2, b2):
            S, B, _ = x.shape
            xf = x.reshape(S * B, D)
            logits = xf @ Wg.T
            idx = jnp.argmax(logits, axis=-1)
            out = jnp.zeros_like(xf)
            for e in range(E):
                m = (idx == e)[:, None].astype(xf.dtype)
                h = jax.nn.relu(xf @ W1[e] + b1[e])
                out = out + m * (h @ W2[e] + b2[e])
            return out.reshape(S, B, D)
        y = _layer_norm(x + _mha(x, Wqkv, bqkv, Wo, bo), g1, be1)
        z = _layer_norm(y + _moe(y, Wg, W1, b1, W2, b2), g2, be2)
        return z
    x = L0_attn_a_x
    x = x + _L0_attn_a_ref(_layernorm(x, axis=-1), L0_attn_a_Wq, L0_attn_a_bq, L0_attn_a_Wk, L0_attn_a_bk, L0_attn_a_Wv, L0_attn_a_bv, L0_attn_a_Wo, L0_attn_a_bo, L0_attn_a_W1, L0_attn_a_b1, L0_attn_a_W2, L0_attn_a_b2, L0_attn_a_g1, L0_attn_a_beta1, L0_attn_a_g2, L0_attn_a_beta2)
    x = x + _L0_ffn_ref(_layernorm(x, axis=-1), L0_ffn_Wqkv, L0_ffn_bqkv, L0_ffn_Wo, L0_ffn_bo, L0_ffn_g1, L0_ffn_be1, L0_ffn_g2, L0_ffn_be2, L0_ffn_Wg, L0_ffn_W1, L0_ffn_b1, L0_ffn_W2, L0_ffn_b2)
    x = x + _L0_attn_b_ref(_layernorm(x, axis=-1), L0_attn_b_Wq, L0_attn_b_bq, L0_attn_b_Wk, L0_attn_b_bk, L0_attn_b_Wv, L0_attn_b_bv, L0_attn_b_Wo, L0_attn_b_bo)
    x = x + _L0_ffn_ref(_layernorm(x, axis=-1), L0_ffn_Wqkv, L0_ffn_bqkv, L0_ffn_Wo, L0_ffn_bo, L0_ffn_g1, L0_ffn_be1, L0_ffn_g2, L0_ffn_be2, L0_ffn_Wg, L0_ffn_W1, L0_ffn_b1, L0_ffn_W2, L0_ffn_b2)
    return x

_drawn_inputs = setup_inputs


def setup_inputs(seed=0):
    import zlib

    import numpy as np

    out = dict(_drawn_inputs(seed))
    spreads = {'L0_attn_a_bq': (0.0, 2.0),
     'L0_attn_a_bk': (0.0, 2.0),
     'L0_attn_a_bv': (0.0, 0.1),
     'L0_attn_a_bo': (0.0, 0.1),
     'L0_attn_a_b1': (0.0, 0.1),
     'L0_attn_a_b2': (0.0, 0.1),
     'L0_attn_a_g1': (1.0, 0.2),
     'L0_attn_a_beta1': (0.0, 0.1),
     'L0_attn_a_g2': (1.0, 0.2),
     'L0_attn_a_beta2': (0.0, 0.1),
     'L0_attn_b_bq': (0.0, 0.1),
     'L0_attn_b_bk': (0.0, 0.1),
     'L0_attn_b_bv': (0.0, 0.1),
     'L0_ffn_bqkv': (0.0, 0.1),
     'L0_ffn_bo': (0.0, 0.1),
     'L0_ffn_g1': (1.0, 0.2),
     'L0_ffn_be1': (0.0, 0.1),
     'L0_ffn_g2': (1.0, 0.2),
     'L0_ffn_be2': (0.0, 0.1),
     'L0_ffn_b1': (0.0, 0.1),
     'L0_ffn_b2': (0.0, 0.1)}
    factors = {'L0_attn_b_bo': 8.0}
    for name, (base, spread) in spreads.items():
        noise = np.random.default_rng([zlib.crc32(name.encode()), seed]).standard_normal(out[name].shape)
        drawn = base * np.exp(spread * noise) if base else spread * noise
        out[name] = jnp.asarray(drawn.astype(out[name].dtype))
    for name, factor in factors.items():
        out[name] = (out[name] * factor).astype(out[name].dtype)
    return out
```

```python
from contextlib import ExitStack, contextmanager

import numpy as np
import concourse.bass as bass
from concourse import mybir

F32 = mybir.dt.float32
I32 = mybir.dt.int32
U32 = mybir.dt.uint32
ALU = mybir.AluOpType
ACT = mybir.ActivationFunctionType
AX = mybir.AxisListType

P = 128
D = 128
S, B = 16, 256
T = S * B
NT = T // P
PAIRS = NT // 2
HA = 16
HM, DM = 4, 32
HB, DB = 16, 64
F = 512
FC = F // P
E = 8
ET = (T + E * (P - 1)) // P
EW = F + F + D
HAT = 0.125
ROW = 1.0 / (D * HAT)
EPS = 1e-5
FAR = -1e30


def pipeline(eng, n, depth, unroll, body, first):
    assert first >= depth - 1 and (n - first) % unroll == 0

    def peeled(i):
        body(i, i, lambda k: 0 <= i - k < n, lambda k: (i - k) // unroll)
    for i in range(first):
        peeled(i)
    if n > first:
        with eng.Fori(0, (n - first) // unroll) as j:
            for u in range(first, first + unroll):
                body(j * unroll + u, u, lambda k: True, lambda k: j + (u - k) // unroll)
    for i in range(n, n + depth - 1):
        peeled(i)


def after(eng, sem, count):
    if not (isinstance(count, int) and count <= 0):
        eng.wait_ge(sem, count)


def build(nc, A, out):
    ctx = ExitStack()
    with ctx:
        def sb(name, shape, dt=F32):
            return ctx.enter_context(nc.sbuf_tensor(name, shape, dt))

        def sem(name):
            return ctx.enter_context(nc.semaphore(name))

        bank = [ctx.enter_context(nc.psum_tensor(f"bank{b}", [P, 512], F32)) for b in range(4)]
        wide = ctx.enter_context(nc.psum_tensor("wide", [P, 2048], F32))
        bank += [wide[:, 512 * b:512 * (b + 1)] for b in range(4)]

        x1_dram = nc.dram_tensor("x1_dram", [T, D], F32)
        x2_dram = nc.dram_tensor("x2_dram", [T, D], F32)
        x3_dram = nc.dram_tensor("x3_dram", [T, D], F32)
        sorted_dram = [nc.dram_tensor(f"sorted{n}_dram", [ET * P, D], F32) for n in range(2)]
        moved_dram = [nc.dram_tensor(f"moved{n}_dram", [ET * P, D], F32) for n in range(2)]

        ident = sb("ident", [P, P])
        zero = sb("zero", [P, P])
        spread = sb("spread", [1, P])
        half_neg = sb("half_neg", [P, 8])
        half = sb("half", [P, 2, 6])
        minus1 = sb("minus1", [P, 1])
        hats = sb("hats", [P, 2, D])
        blk8 = sb("blk8", [P, P])
        far = sb("far", [P, 32])
        lower = sb("lower", [P, P])
        ones = sb("ones", [P, P])
        rank_w = sb("rank_w", [P, E])
        upto = sb("upto", [P, E, E])
        steps = sb("steps", [P, NT])
        tile_no = sb("tile_no", [P, ET])
        resets = sb("resets", [P, E * NT])

        wa_qkv = sb("wa_qkv", [P, 3 * D])
        wa_o = sb("wa_o", [P, D])
        ra0 = sb("ra0", [P, D])
        wa1 = sb("wa1", [P, F])
        wa2 = sb("wa2", [P, FC, D])
        ra1 = sb("ra1", [P, D])
        col = sb("col", [P, 4])
        col16 = sb("col16", [P, 4])
        g2a, b2a = sb("g2a", [P, D]), sb("b2a", [P, D])
        g2f, b2f = sb("g2f", [P, D]), sb("b2f", [P, D])
        wg_raw = sb("wg_raw", [E, D])
        wf_qkv = sb("wf_qkv", [P, 3 * D])
        wf_o = sb("wf_o", [P, D])
        wg_t = sb("wg_t", [P, E])
        wg = sb("wg", [P, E])
        rf0 = sb("rf0", [P, D])
        we = sb("we", [P, E, EW])
        ident4 = ident[:, :].unsqueeze(1).to_broadcast([P, 4, P])
        wb_o = sb("wb_o", [P, HB // 2, D])
        qk_t = sb("qk_t", [P, HB, D])
        vo = sb("vo", [P, HB, D])

        xa = sb("xa", [P, NT, D])
        z1_all = sb("z1_all", [P, NT, D])
        stats = sb("stats", [P, 3, 6, 6])
        both_m = sb("both_m", [P, 3, 2, 6])
        mean = sb("mean", [P, 3, 2, 6])
        spread_m = sb("spread_m", [P, 3, 2, 6])
        rstd = sb("rstd", [P, 3, 6])
        z0 = sb("z0", [P, 3, 2, D])
        z1 = sb("z1", [P, 3, 2, D])
        zt = sb("zt", [P, 3, 2, 2 * P])
        q_t = sb("q_t", [P, 3, 2 * P])
        v_r = sb("v_r", [P, 3, 2, P + 2])
        att_t = sb("att_t", [P, 3, 2 * P])
        tmp = sb("tmp", [P, 3, 2, D])
        xout = sb("xout", [P, 3, 2, D])
        sc = sb("sc", [P, 3, 2, HM, 32])
        mx = sb("mx", [P, 3, 2 * HM])
        sums = sb("sums", [P, 3, 2 * HM])
        inv = sb("inv", [P, 3, 2 * HM])
        logit = sb("logit", [P, NT, E])
        cnt = sb("cnt", [P, E])
        tot = sb("tot", [P, 2 * E])
        n_tiles = sb("n_tiles", [P, E])
        ends = sb("ends", [P, E])
        base = sb("base", [P, E])
        pos_f = sb("pos_f", [P, NT])
        pos = sb("pos", [P, NT], U32)
        owner_f = sb("owner_f", [P, ET])
        owner = sb("owner", [P, ET], I32)
        var_e = sb("var_e", [P, 3, 1])
        mv = sb("mv", [P, 3, 2])
        zs = sb("zs", [P, 3, D])
        gram = sb("gram", [P, 3, P])
        m_sb = sb("m_sb", [P, 3, D])

        early = sb("early", [P, 6144])
        late = sb("late", [P, 6144])
        rows_f = sb("rows_f", [P, 2048])
        hid_f = sb("hid_f", [P, 2048])

        def parts(whole, *shapes):
            at, cut = 0, []
            for shape in shapes:
                size = int(np.prod(shape))
                part = whole[:, at:at + size]
                names = "abcdef"[:len(shape)]
                if len(shape) > 1:
                    part = part.rearrange(f"p ({' '.join(names)}) -> p {' '.join(names)}",
                                          **dict(zip(names[1:], shape[1:])))
                cut.append(part)
                at += size
            assert at <= whole.shape[1], at
            return cut

        wb_t, wa_raw, wa1_raw, wf_raw, wf_t, wfo_raw, row_a2, centre, fold_a, fold_f = parts(
            early, (3, HB // 2, D), (3 * D,), (F,), (3, D), (3 * D,), (D,), (D + F + D,), (P,), (P,), (P,))
        wb_raw, row_b = parts(late, (3, HB * DB), (3 * HB * DB,))
        row_b2, row_f, row_bo, row_a = (r[0:1] for r in parts(rows_f, (E * D,), (4 * D,), (D,), (3 * D,)))
        row_b1 = z1_all[0:1, :, :].rearrange("p t d -> p (t d)")
        row_b, row_a2 = row_b[0:1], row_a2[0:1]
        k_r, exp_q, exp_k, kv, den, xres = parts(
            early[:, 0:3072], (2, 2, P), (2, 2 * P), (2, 2, P), (2, 2, P), (2, 2 * P), (2, 2, D))
        hid, = parts(hid_f, (2, FC, 2 * P))
        k_x, p_t = parts(early, (3, 2, 4, HM, 32), (3, 2, HM, P))
        we_t, hot, hot_inc, over, place, seen, owner_m, best, ends_m = parts(
            late, (3, EW), (E, NT), (E, NT), (E, NT), (E, NT), (NT, E), (ET, E), (NT,), (E, E))
        hid_e, = parts(hid_f, (3, FC, P))
        u_sb, = parts(late, (3, HB * D))

        blk16 = att_t[:, 0, 0:P]

        consts_made = sem("consts_made")
        const_step = sem("const_step")
        stats_init = sem("stats_init")

        programs = {"sync": [], "gpsimd": [], "scalar": [], "vector": [], "tensor": []}

        def on(engine):
            def add(f):
                programs[engine].append(f)
                return f
            return add

        @on("gpsimd")
        def _(pool):
            nc.gpsimd.memset(zero[:, :], 0.0).then_inc(const_step, 1)
            nc.gpsimd.memset(ones[:, :], 1.0).then_inc(const_step, 1)
            nc.gpsimd.memset(spread[:, :], ROW).then_inc(const_step, 1)
            nc.gpsimd.memset(half_neg[:, :], -0.5).then_inc(const_step, 1)
            nc.gpsimd.memset(hats[:, :, :], HAT)
            nc.gpsimd.memset(minus1[:, :], -1.0)
            nc.gpsimd.memset(half[:, :, :], 0.5)
            nc.gpsimd.memset(stats[:, :, :, :], 1.0).then_inc(stats_init, 1)
            nc.gpsimd.memset(resets[:, :], 1.0).then_inc(const_step, 1)
            pool.wait_ge(const_step, 5)

            def select(out_, in_, pattern, base, mult, op, fill):
                return nc.gpsimd.affine_select(out=out_, in_=in_, compare_op=op, fill=fill, base=base,
                                               pattern=pattern, channel_multiplier=mult)
            select(ident[:, :], zero[:, :], [[-1, P]], 0, 1, ALU.not_equal, 1.0).then_inc(const_step, 1)
            select(lower[:, :], ones[:, :], [[1, P]], 0, -1, ALU.is_gt, 0.0).then_inc(const_step, 1)
            select(blk8[:, :], ones[:, :], [[-8, HA], [0, 8]], 0, 1, ALU.is_ge, 0.0).then_inc(const_step, 1)
            pool.wait_ge(const_step, 8)
            select(blk8[:, :], blk8[:, :], [[8, HA], [0, 8]], 7, -1, ALU.is_ge, 0.0).then_inc(const_step, 1)
            nc.gpsimd.tensor_scalar(centre[:, :], ident[:, :], 1.0, -1.0 / D, ALU.mult, ALU.add).then_inc(const_step, 1)
            nc.gpsimd.iota(rank_w[:, :], [[-1, E]], base=E, channel_multiplier=0,
                           allow_small_or_imprecise_dtypes=True).then_inc(const_step, 1)
            nc.gpsimd.iota(steps[:, :], [[P, NT]], base=0, channel_multiplier=0,
                           allow_small_or_imprecise_dtypes=True).then_inc(const_step, 1)
            nc.gpsimd.iota(tile_no[:, :], [[1, ET]], base=0, channel_multiplier=0,
                           allow_small_or_imprecise_dtypes=True).then_inc(const_step, 1)
            select(upto[:, :, :], ones[:, 0:E * E].rearrange("p (e f) -> p e f", e=E), [[1, E], [-1, E]], 0, 0,
                   ALU.is_ge, 0.0).then_inc(const_step, 1)
            nc.gpsimd.memset(resets[:, :].rearrange("p (e t) -> p e t", e=E)[:, :, 0], 0.0).then_inc(const_step, 1)
            select(blk16, ones[:, :], [[-16, 8], [0, 16]], 0, 1, ALU.is_ge, 0.0).then_inc(const_step, 1)
            pool.wait_ge(const_step, 16)
            select(blk16, blk16, [[16, 8], [0, 16]], 15, -1, ALU.is_ge, 0.0).then_inc(const_step, 1)
            pool.wait_ge(const_step, 17)
            nc.gpsimd.memset(z0[0:1, 0, 0, 0:1], 0.0).then_inc(consts_made, 1)

        w_a_in = sem("w_a_in")
        w_o_in = sem("w_o_in")
        zeros_out = sem("zeros_out")

        def row(v):
            return v.rearrange("(a n) -> a n", a=1)

        def column(v):
            return v.rearrange("(n a) -> n a", a=1)

        X_PARTS = ((0, 2), (2, 8), (8, 16), (16, 24), (24, 32))
        x_in = [sem(f"x_in{n}") for n in range(len(X_PARTS))]
        a = {n[10:]: A[n] for n in A if n.startswith("L0_attn_a_")}
        f = {n[7:]: A[n] for n in A if n.startswith("L0_ffn_")}
        b = {n[10:]: A[n] for n in A if n.startswith("L0_attn_b_")}
        loads_a = [(wa_raw[:, 0:D], a["Wq"]), (wa_raw[:, D:2 * D], a["Wk"]), (wa_raw[:, 2 * D:], a["Wv"]),
                   (row_a[:, 0:D], row(a["bq"])), (row_a[:, D:2 * D], row(a["bk"])), (row_a[:, 2 * D:], row(a["bv"])),
                   (row_a2[:, 0:D], row(a["bo"])), (row_a2[:, D:D + F], row(a["b1"])), (row_a2[:, D + F:], row(a["b2"])),
                   (wa_o[:, :], a["Wo"]), (wa1_raw[:, :], a["W1"]),
                   (wa2[:, :, :], a["W2"].rearrange("(c p) d -> p c d", p=P)),
                   (col[:, 0:1], column(a["g1"])), (col[:, 1:2], column(a["beta1"])),
                   (col[:, 2:3], column(f["g1"])), (col[:, 3:4], column(f["be1"])),
                   (g2a[:, :], row(a["g2"]).to_broadcast([P, D])), (b2a[:, :], row(a["beta2"]).to_broadcast([P, D]))]
        loads_o = [(wf_raw[:, :, :], f["Wqkv"].rearrange("(c p) d -> p c d", p=P)), (wfo_raw[:, :], f["Wo"]),
                   (wg_raw[:, :], f["Wg"]), (row_f[:, 0:3 * D], row(f["bqkv"])), (row_f[:, 3 * D:], row(f["bo"])),
                   (row_b1[:, :], f["b1"].rearrange("(a e) n -> a (e n)", a=1)),
                   (row_b2[:, :], f["b2"].rearrange("(a e) n -> a (e n)", a=1)),
                   (g2f[:, :], row(f["g2"]).to_broadcast([P, D])), (b2f[:, :], row(f["be2"]).to_broadcast([P, D]))]
        loads_o += [(we[:, e, 0:F], f["W1"][e]) for e in range(E)]
        loads_o += [(we[:, e, F:2 * F].rearrange("p (c d) -> p c d", c=FC),
                     f["W2"][e].rearrange("(c p) d -> p c d", p=P)) for e in range(E)]
        loads_o += [(row_b[:, 0:1024], row(b["bq"])), (row_b[:, 1024:2048], row(b["bk"])),
                    (row_b[:, 2048:], row(b["bv"])), (row_bo[:, :], row(b["bo"])),
                    (wb_raw[:, 0, :], b["Wq"]), (wb_raw[:, 1, :], b["Wk"]), (wb_raw[:, 2, :], b["Wv"]),
                    (wb_o[:, :, :], b["Wo"].rearrange("(c p) d -> p c d", p=P))]

        @on("sync")
        def _(sp):
            xs = a["x"].rearrange("s (h p) d -> p (s h) d", p=P)
            for n, (lo, hi) in enumerate(X_PARTS):
                sp.dma_start(xa[:, lo:hi, :], xs[:, lo:hi, :]).then_inc(x_in[n], 16)
                if n == 0:
                    for dst, src in loads_a:
                        sp.dma_start(dst, src).then_inc(w_a_in, 16)
            for dst, src in loads_o:
                sp.dma_start(dst, src).then_inc(w_o_in, 16)
            sp.wait_ge(consts_made, 1)
            for d in sorted_dram:
                for t in range(ET):
                    sp.dma_start(d[t * P:(t + 1) * P, :], zero[:, :]).then_inc(zeros_out, 16)
        ZEROS = 16 * 2 * ET

        rows_made = sem("rows_made")
        fold_step = sem("fold_step")
        folds_made = sem("folds_made")
        hat_done = sem("hat_done")
        hat_kept = sem("hat_kept")
        ones_col = sem("ones_col")
        off_blocks = sem("off_blocks")

        @on("vector")
        def _(dve):
            dve.wait_ge(w_a_in, 16 * len(loads_a))
            dve.wait_ge(consts_made, 1)
            nc.vector.tensor_scalar_add(row_a[0:1, 0:2 * D], row_a[0:1, 0:2 * D], 1.0).then_inc(rows_made, 1)
            nc.vector.tensor_scalar_mul(col16[:, :], col[:, :], ROW).then_inc(fold_step, 1)
            dve.wait_ge(fold_step, 1)
            nc.vector.tensor_scalar(fold_a[:, :], centre[:, :], col[:, 0:1], col16[:, 1:2], ALU.mult, ALU.add)
            nc.vector.tensor_scalar(fold_f[:, :], centre[:, :], col[:, 2:3], col16[:, 3:4], ALU.mult,
                                    ALU.add).then_inc(folds_made, 1)
            nc.vector.tensor_reduce(out=far[:, :], in_=blk16.rearrange("p (q c) -> p c q", q=4), axis=AX.X,
                                    op=ALU.add).then_inc(fold_step, 1)
            dve.wait_ge(fold_step, 2)
            nc.vector.tensor_scalar(far[:, :], far[:, :], -1.0, -FAR, ALU.add, ALU.mult).then_inc(fold_step, 1)
            nc.vector.memset(v_r[:, :, :, P:P + 1], 1.0).then_inc(ones_col, 1)

        HAT_BANK = (4, 5)

        def hat(width, lhsT, rhs, bias, dst, **kw):
            return dict(width=width, parts=[(0, width, [(lhsT, rhs)] + ([(spread[:, :], bias)] if bias is not None else []))],
                        dst=dst, **kw)

        hats_a = [hat(3 * D, centre[:, :], wa_raw[:, :], row_a[:, :], wa_qkv[:, :]),
                  hat(D, centre[:, :], ident[:, :], row_a2[:, 0:D], ra0[:, :]),
                  hat(F, fold_a[:, :], wa1_raw[:, :], row_a2[:, D:D + F], wa1[:, :]),
                  hat(D, fold_a[:, :], ident[:, :], row_a2[:, D + F:], ra1[:, :])]
        N_A = len(hats_a)
        turned = [dict(width=3 * D, turns=[(n * D, wf_raw[:, n, :], ident[:, :]) for n in range(3)], dst=wf_t[:, :]),
                  dict(width=D, turns=[(0, wfo_raw[:, :], ident[:, :])], dst=wf_o[:, :]),
                  dict(width=E, turns=[(0, wg_raw[:, :], ident[0:E, 0:E])], dst=wg_t[:, :])]
        hats_f = turned + [hat(3 * D, centre[:, :], wf_t[:, :], row_f[:, 0:3 * D], wf_qkv[:, :], after=N_A + 1),
                           hat(D, centre[:, :], ident[:, :], row_f[:, 3 * D:], rf0[:, :]),
                           hat(E, fold_f[:, :], wg_t[:, :], None, wg[:, :], after=N_A + 3)]
        hats_f += [hat(F, fold_f[:, :], we[:, e, 0:F], row_b1[:, e * F:(e + 1) * F], we[:, e, 0:F]) for e in range(E)]
        hats_f += [hat(4 * D, fold_f[:, :], ident4, row_b2[:, e * D:(e + 4) * D], we[:, e:e + 4, 2 * F:])
                   for e in (0, 4)]
        hats_b = [dict(width=4 * P, dst=wb_t[:, m, c:c + 4, :],
                       parts=[(n * P, P, [(wb_raw[:, m, (c + n) * P:(c + n + 1) * P], centre[:, :]),
                                          (row_b[:, 1024 * m + (c + n) * P:1024 * m + (c + n + 1) * P], spread[:, :])])
                              for n in range(4)]) for m in range(3) for c in (0, 4)]
        N_T = N_A + len(hats_f) + len(hats_b)
        for h0 in (0, 1, 8, 9):
            lo = DB * (h0 % 2)
            hats_b.append(dict(width=4 * P, dst=qk_t[:, h0:h0 + 7:2, :], after=N_T,
                               parts=[(n * P, P, [(wb_t[lo:lo + DB, 1, h0 // 2 + n, :], wb_t[lo:lo + DB, 0, h0 // 2 + n, :])])
                                      for n in range(4)]))
        for h0 in (0, 1, 8, 9):
            lo = DB * (h0 % 2)
            hats_b.append(dict(width=4 * P, dst=vo[:, h0:h0 + 7:2, :], scale=DB ** -0.5,
                               parts=[(n * P, P, [(wb_t[lo:lo + DB, 2, h0 // 2 + n, :], wb_o[lo:lo + DB, h0 // 2 + n, :])])
                                      for n in range(4)]))
        N_HATS = N_A + len(hats_f) + len(hats_b)

        def hat_products(pe, jobs, first):
            for n, job in enumerate(jobs, first):
                to = bank[HAT_BANK[n % 2]]
                after(pe, hat_kept, max(n - 1, job.get("after", 0)))
                for at, lhsT, eye in job.get("turns", []):
                    last = nc.tensor.transpose(to[:, at:at + lhsT.shape[0]], lhsT, eye)
                for at, w, factors in job.get("parts", []):
                    for m, (lhsT, rhs) in enumerate(factors):
                        last = nc.tensor.matmul(to[:, at:at + w], lhsT, rhs, start=(m == 0), stop=(m == len(factors) - 1))
                last.then_inc(hat_done, 1)

        def hat_copies(act, jobs, first):
            for n, job in enumerate(jobs, first):
                act.wait_ge(hat_done, n + 1)
                src = bank[HAT_BANK[n % 2]][:, 0:job["width"]]
                dst = job["dst"]
                if len(dst.shape) == 3:
                    src = src.rearrange("p (n d) -> p n d", n=dst.shape[1])
                nc.scalar.activation(dst, src, ACT.Copy, scale=job.get("scale", 1.0)).then_inc(hat_kept, 1)

        @on("tensor")
        def _(pe):
            pe.wait_ge(consts_made, 1)
            pe.wait_ge(w_a_in, 16 * len(loads_a))
            pe.wait_ge(rows_made, 1)
            pe.wait_ge(folds_made, 1)
            hat_products(pe, hats_a, 0)

        @on("scalar")
        def _(act):
            hat_copies(act, hats_a, 0)

        def tile(x, n):
            return x[:, bass.ds(n, 1), :].rearrange("p a d -> p (a d)")

        def both(x, n):
            return x[:, bass.ds(n * 2, 2), :]

        def bn(sources, slot, at, done):
            for n, x in enumerate(sources):
                last = nc.vector.bn_stats(stats[:, slot, at + n, :], x)
            last.then_inc(done, 1)

        def roots(pool, slot, body_no, width, made, step, rstd_made):
            st, w = stats[:, slot], slice(0, width)
            for sem_, count in made:
                pool.wait_ge(sem_, count)
            nc.gpsimd.tensor_tensor(both_m[:, slot, 0, w], st[:, w, 1], st[:, w, 4], ALU.add)
            nc.gpsimd.tensor_tensor(both_m[:, slot, 1, w], st[:, w, 1], st[:, w, 4], ALU.subtract)
            nc.gpsimd.tensor_tensor(spread_m[:, slot, 0, w], st[:, w, 2], st[:, w, 5], ALU.add).then_inc(step, 1)
            pool.wait_ge(step, body_no * 4 + 1)
            nc.gpsimd.tensor_tensor(mean[:, slot, :, w], both_m[:, slot, :, w], half[:, :, w], ALU.mult)
            nc.gpsimd.tensor_scalar(spread_m[:, slot, 1, w], spread_m[:, slot, 0, w], 1.0 / D, EPS, ALU.mult,
                                    ALU.add).then_inc(step, 1)
            pool.wait_ge(step, body_no * 4 + 2)
            nc.gpsimd.tensor_tensor(spread_m[:, slot, 0, w], mean[:, slot, 1, w], mean[:, slot, 1, w],
                                    ALU.mult).then_inc(step, 1)
            pool.wait_ge(step, body_no * 4 + 3)
            nc.gpsimd.tensor_tensor(spread_m[:, slot, 0, w], spread_m[:, slot, 0, w], spread_m[:, slot, 1, w],
                                    ALU.add).then_inc(step, 1)
            pool.wait_ge(step, body_no * 4 + 4)
            nc.gpsimd.tensor_tensor(rstd[:, slot, w], spread_m[:, slot, 0, w], half_neg[:, w],
                                    ALU.pow).then_inc(rstd_made, 1)

        def normalise(dst, src, slot, at):
            return nc.vector.tensor_scalar(dst, src, mean[:, slot, 0, at:at + 1], rstd[:, slot, at:at + 1],
                                           ALU.subtract, ALU.mult)

        a_s = {n: sem("a_" + n) for n in (
            "stats0", "stats1", "stats2", "step", "rstd", "z0", "z1", "turned", "zt", "kv_rows", "q_cols",
            "exp_q", "v", "phi", "sums", "masked", "att", "den", "inv", "att_t", "wo", "hid_a", "hid_b",
            "relu_a", "relu_b", "w2", "xres", "tmp", "x1")}
        a_stored = [sem(f"a_stored{n}") for n in range(2)]
        A_DEPTH, A_FIRST = 7, 8
        TT, QM, KV, ND, WO, W2B = bank[0], bank[1], bank[2], bank[3], bank[6], bank[7]
        WH = wide[:, 0:1024]

        @on("tensor")
        def _(pe):
            g = a_s
            pe.wait_ge(hat_kept, N_A)
            pe.wait_ge(ones_col, 1)

            def body(i, s, has, lap):
                c, l = s % 2, (s - 1) % 2
                if has(3):
                    pe.wait_ge(g["att_t"], i - 2)
                    after(pe, g["z1"], i - 3)
                    for t in range(2):
                        cut = slice(t * P, (t + 1) * P)
                        nc.tensor.matmul(WO[:, cut], att_t[:, l, cut], wa_o[:, :], start=True, stop=False)
                        last = nc.tensor.matmul(WO[:, cut], zt[:, l, 0, cut], ra0[:, :], start=False, stop=True)
                    last.then_inc(g["wo"], 1)
                if has(2):
                    pe.wait_ge(g["v"], i - 1)
                    pe.wait_ge(g["phi"], i - 1)
                    for t in range(2):
                        last = nc.tensor.matmul(QM[:, 256:256 + P + 1], k_r[:, c, t, :], v_r[:, c, t, 0:P + 1],
                                                start=(t == 0), stop=(t == 1))
                    last.then_inc(g["sums"], 1)
                if has(1) or has(4):
                    after(pe, g["zt"], i - 1)
                    if has(1):
                        pe.wait_ge(g["z0"], i)
                        for t in range(2):
                            last = nc.tensor.transpose(TT[:, t * P:(t + 1) * P], z0[:, l, t, :], ident[:, :])
                    if has(4):
                        pe.wait_ge(g["z1"], i - 3)
                        for t in range(2):
                            last = nc.tensor.transpose(TT[:, 256 + t * P:256 + (t + 1) * P], z1[:, l, t, :], ident[:, :])
                    last.then_inc(g["turned"], 1)
                if has(1):
                    pe.wait_ge(g["zt"], i)
                    for t in range(2):
                        last = nc.tensor.matmul(KV[:, t * 256:(t + 1) * 256], zt[:, l, 0, t * P:(t + 1) * P],
                                                wa_qkv[:, D:3 * D], start=True, stop=True)
                    last.then_inc(g["kv_rows"], 1)
                    if has(2):
                        pe.wait_ge(g["masked"], i - 1)
                    nc.tensor.matmul(QM[:, 0:256], wa_qkv[:, 0:D], zt[:, l, 0, :], start=True,
                                     stop=True).then_inc(g["q_cols"], 1)
                if has(2):
                    pe.wait_ge(g["masked"], i - 1)
                    after(pe, g["att_t"], i - 2)
                    nc.tensor.matmul(ND[:, 0:256], kv[:, c, 0, :], q_t[:, c, :], start=True, stop=True)
                    nc.tensor.matmul(ND[:, 256:512], kv[:, c, 1, :], q_t[:, c, :], start=True,
                                     stop=True).then_inc(g["att"], 1)
                if has(4):
                    if not has(1):
                        pe.wait_ge(g["zt"], i)
                    for m in range(FC):
                        if m == 0:
                            after(pe, g["relu_a"], i - 4)
                        if m == 2:
                            after(pe, g["relu_b"], i - 4)
                        last = nc.tensor.matmul(WH[:, m * 256:(m + 1) * 256], wa1[:, m * P:(m + 1) * P],
                                                zt[:, l, 1, :], start=True, stop=True)
                        if m == 1:
                            last.then_inc(g["hid_a"], 1)
                    last.then_inc(g["hid_b"], 1)
                if has(5):
                    pe.wait_ge(g["relu_a"], i - 4)
                    pe.wait_ge(g["relu_b"], i - 4)
                    after(pe, g["tmp"], i - 5)
                    for t in range(2):
                        cut = slice(t * P, (t + 1) * P)
                        for m in range(FC):
                            nc.tensor.matmul(W2B[:, cut], hid[:, l, m, cut], wa2[:, m, :], start=(m == 0), stop=False)
                        last = nc.tensor.matmul(W2B[:, cut], zt[:, c, 1, cut], ra1[:, :], start=False, stop=True)
                    last.then_inc(g["w2"], 1)
            pipeline(pe, PAIRS, A_DEPTH, 2, body, A_FIRST)

        @on("scalar")
        def _(act):
            g = a_s

            def body(i, s, has, lap):
                c, l = s % 2, (s - 1) % 2
                if has(1) or has(4):
                    act.wait_ge(g["turned"], i)
                    lo, hi = (0 if has(1) else 1), (2 if has(4) else 1)
                    nc.scalar.activation(zt[:, l, lo:hi, :], TT[:, 256 * lo:256 * hi].rearrange("p (n t) -> p n t", n=hi - lo),
                                         ACT.Copy, bias=HAT).then_inc(g["zt"], 1)
                if has(1):
                    act.wait_ge(g["kv_rows"], i)
                    rows = KV[:, :].rearrange("p (t n) -> p t n", t=2)
                    nc.scalar.activation(exp_k[:, l, :, :], rows[:, :, 0:P], ACT.Exp, bias=minus1[:, 0:1])
                    nc.scalar.activation(v_r[:, l, :, 0:P], rows[:, :, P:2 * P], ACT.Copy).then_inc(g["v"], 1)
                    act.wait_ge(g["q_cols"], i)
                    nc.scalar.activation(exp_q[:, l, :], QM[:, 0:256], ACT.Exp, bias=minus1[:, 0:1]).then_inc(g["exp_q"], 1)
                if has(2):
                    act.wait_ge(g["att"], i - 1)
                    nc.scalar.activation(den[:, c, :], ND[:, 256:512], ACT.Copy, bias=1e-6).then_inc(g["den"], 1)
                if has(4):
                    act.wait_ge(g["hid_a"], i - 3)
                    nc.scalar.activation(hid[:, c, 0:2, :], WH[:, 0:512].rearrange("p (m t) -> p m t", m=2),
                                         ACT.Relu).then_inc(g["relu_a"], 1)
            act.wait_ge(ones_col, 1)
            pipeline(act, PAIRS, A_DEPTH, 2, body, A_FIRST)

        @on("vector")
        def _(dve):
            g = a_s

            def body(i, s, has, lap):
                c, l = s % 2, (s - 1) % 2
                if has(6):
                    dve.wait_ge(g["w2"], i - 5)
                    bn([W2B[:, 0:P], W2B[:, P:2 * P]], c, 4, g["stats2"])
                if has(0):
                    if isinstance(i, int):
                        for n, (lo, hi) in enumerate(X_PARTS):
                            if lo <= 2 * i < hi or (i == A_FIRST - 1 and lo > 2 * i):
                                dve.wait_ge(x_in[n], 16)
                    bn([tile(xa, i * 2), tile(xa, i * 2 + 1)], c, 0, g["stats0"])
                if has(3):
                    dve.wait_ge(g["wo"], i - 2)
                    bn([WO[:, 0:P], WO[:, P:2 * P]], c, 2, g["stats1"])
                if has(2):
                    dve.wait_ge(g["sums"], i - 1)
                    nc.vector.tensor_tensor(kv[:, c, 0, :], QM[:, 256:256 + P], blk8[:, :], ALU.mult)
                    nc.vector.tensor_scalar(kv[:, c, 1, :], blk8[:, :], QM[:, 256 + P:256 + P + 1], None,
                                            ALU.mult).then_inc(g["masked"], 1)
                dve.wait_ge(g["rstd"], i + 1)
                if has(3):
                    for t in range(2):
                        last = normalise(z1[:, c, t, :], WO[:, t * P:(t + 1) * P], c, 2 + t)
                    last.then_inc(g["z1"], 1)
                if has(6):
                    for t in range(2):
                        last = nc.vector.scalar_tensor_tensor(out=tmp[:, c, t, :], in0=W2B[:, t * P:(t + 1) * P],
                                                              scalar=mean[:, c, 0, 4 + t:5 + t], in1=g2a[:, :],
                                                              op0=ALU.subtract, op1=ALU.mult)
                    last.then_inc(g["tmp"], 1)
                if has(0):
                    for t in range(2):
                        last = normalise(z0[:, c, t, :], tile(xa, i * 2 + t), c, t)
                    last.then_inc(g["z0"], 1)
                if has(6):
                    dve.wait_ge(g["tmp"], i - 5)
                    dve.wait_ge(g["xres"], i - 5)
                    after(dve, a_stored[c], lap(8) * 16 + 16)
                    for t in range(2):
                        last = nc.vector.scalar_tensor_tensor(out=xout[:, c, t, :], in0=tmp[:, c, t, :],
                                                              scalar=rstd[:, c, 4 + t:5 + t], in1=xres[:, c, t, :],
                                                              op0=ALU.mult, op1=ALU.add)
                    last.then_inc(g["x1"], 1)
                if has(1):
                    dve.wait_ge(g["v"], i)
                    rows = KV[:, :].rearrange("p (t n) -> p t n", t=2)
                    nc.vector.scalar_tensor_tensor(out=k_r[:, l, :, :], in0=exp_k[:, l, :, :], scalar=1.0,
                                                   in1=rows[:, :, 0:P], op0=ALU.min, op1=ALU.max)
                    dve.wait_ge(g["exp_q"], i)
                    nc.vector.scalar_tensor_tensor(out=q_t[:, l, :], in0=exp_q[:, l, :], scalar=1.0,
                                                   in1=QM[:, 0:256], op0=ALU.min, op1=ALU.max).then_inc(g["phi"], 1)
                if has(2):
                    dve.wait_ge(g["den"], i - 1)
                    nc.vector.reciprocal(den[:, c, :], den[:, c, :]).then_inc(g["inv"], 1)
                    dve.wait_ge(g["inv"], i - 1)
                    nc.vector.tensor_tensor(att_t[:, c, :], ND[:, 0:256], den[:, c, :], ALU.mult).then_inc(g["att_t"], 1)
                if has(4):
                    dve.wait_ge(g["hid_b"], i - 3)
                    nc.vector.tensor_scalar_max(hid[:, c, 2:4, :], WH[:, 512:1024].rearrange("p (m t) -> p m t", m=2),
                                                0.0).then_inc(g["relu_b"], 1)
            dve.wait_ge(stats_init, 1)
            pipeline(dve, PAIRS, A_DEPTH, 2, body, A_FIRST)

        @on("gpsimd")
        def _(pool):
            g = a_s
            pool.wait_ge(w_a_in, 16 * len(loads_a))

            def body(i, s, has, lap):
                c = s % 2
                made = [(g["stats2"], i - 5)] * has(6) + [(g["stats0"], i + 1)] * has(0) + [(g["stats1"], i - 2)] * has(3)
                roots(pool, c, i, 6, made, g["step"], g["rstd"])
                if has(6):
                    after(pool, g["x1"], i - 7)
                    nc.gpsimd.tensor_tensor(xres[:, c, :, :], both(xa, i - 6), b2a[:, :].unsqueeze(1).to_broadcast([P, 2, D]),
                                            ALU.add).then_inc(g["xres"], 1)
            pipeline(pool, PAIRS, A_DEPTH, 2, body, A_FIRST)

        @on("sync")
        def _(sp):
            g = a_s
            rows = x1_dram[:, :].rearrange("(h p s) d -> p h s d", p=P, s=S)

            def body(i, s, has, lap):
                if has(6):
                    sp.wait_ge(g["x1"], i - 5)
                    sp.dma_start(rows[:, :, bass.ds(i - 6, 1), :].rearrange("p h a d -> p h (a d)"),
                                 xout[:, s % 2, :, :]).then_inc(a_stored[s % 2], 16)
            pipeline(sp, PAIRS, A_DEPTH, 2, body, A_FIRST)

        @on("tensor")
        def _(pe):
            pe.wait_ge(w_o_in, 16 * len(loads_o))
            hat_products(pe, hats_f + hats_b, N_A)

        @on("scalar")
        def _(act):
            hat_copies(act, hats_f, N_A)
            act.wait_ge(a_s["x1"], PAIRS)
            hat_copies(act, hats_b, N_A + len(hats_f))

        @on("vector")
        def _(dve):
            dve.wait_ge(hat_kept, N_HATS)
            nc.vector.memset(k_x[:, :, :, :, :, :], 0.0).then_inc(off_blocks, 1)
            nc.vector.memset(p_t[:, :, :, :, :], 0.0).then_inc(off_blocks, 1)

        G_PARTS = 4
        m_s = {k: sem("m_" + k) for k in (
            "stats0", "stats1", "step", "rstd", "z0", "z1", "turned", "zt", "qk", "kx", "v_rows", "v", "s",
            "masked", "max", "centred", "exp", "sum", "inv", "prob", "p_t", "att", "att_t", "wo", "gate", "logit",
            "kept")}
        x_back = [sem(f"m_x{k}") for k in range(G_PARTS)]
        M_BODIES = PAIRS + 4

        def attention_block(n, src_dram, stored_before):
            o, ob = n * PAIRS, n * M_BODIES
            DEPTH, FIRST = 6, 7
            TT, QK, VB, SB, WO, AV, GB = (bank[k] for k in range(7))

            @on("sync")
            def _(sp):
                for sem_, count in stored_before:
                    sp.wait_ge(sem_, count)
                rows = src_dram[:, :].rearrange("(t p) d -> p t d", p=P)
                for k in range(G_PARTS):
                    part = slice(k * NT // G_PARTS, (k + 1) * NT // G_PARTS)
                    sp.dma_start(xa[:, part, :], rows[:, part, :]).then_inc(x_back[k], 16)

            @on("tensor")
            def _(pe):
                g = m_s
                pe.wait_ge(off_blocks, 2)

                def body(i, s, has, lap):
                    c1, c2, c3, c4 = ((s - k) % 3 for k in (1, 2, 3, 4))
                    if has(4):
                        pe.wait_ge(g["att_t"], o + i - 3)
                        after(pe, g["z1"], o + i - 4)
                        for t in range(2):
                            cut = slice(t * P, (t + 1) * P)
                            nc.tensor.matmul(WO[:, cut], att_t[:, c4, cut], wf_o[:, :], start=True, stop=False)
                            last = nc.tensor.matmul(WO[:, cut], zt[:, c4, 0, cut], rf0[:, :], start=False, stop=True)
                        last.then_inc(g["wo"], 1)
                    if has(2):
                        pe.wait_ge(g["kx"], o + i - 1)
                        after(pe, g["masked"], o + i - 2)
                        for t in range(2):
                            for q in range(4):
                                last = nc.tensor.matmul(SB[32 * q:32 * q + 32, t * P:(t + 1) * P],
                                                        q_t[:, c2, t * P + 32 * q:t * P + 32 * q + 32],
                                                        k_x[:, c2, t, q, :, :].rearrange("p h k -> p (h k)"),
                                                        start=True, stop=True)
                        last.then_inc(g["s"], 1)
                    if has(1) or has(5):
                        after(pe, g["zt"], ob + i - 1)
                        if has(1):
                            pe.wait_ge(g["z0"], o + i)
                            for t in range(2):
                                last = nc.tensor.transpose(TT[:, t * P:(t + 1) * P], z0[:, c1, t, :], ident[:, :])
                        if has(5):
                            pe.wait_ge(g["z1"], o + i - 4)
                            for t in range(2):
                                last = nc.tensor.transpose(TT[:, 256 + t * P:256 + (t + 1) * P], z1[:, c2, t, :],
                                                           ident[:, :])
                        last.then_inc(g["turned"], 1)
                    if has(1):
                        pe.wait_ge(g["zt"], ob + i)
                        after(pe, g["kx"], o + i - 1)
                        nc.tensor.matmul(QK[:, 0:256], wf_qkv[:, 0:D], zt[:, c1, 0, :], start=True, stop=True)
                        nc.tensor.matmul(QK[:, 256:512], wf_qkv[:, D:2 * D], zt[:, c1, 0, :], start=True,
                                         stop=True).then_inc(g["qk"], 1)
                        after(pe, g["v"], o + i - 1)
                        for t in range(2):
                            last = nc.tensor.matmul(VB[:, t * P:(t + 1) * P], zt[:, c1, 0, t * P:(t + 1) * P],
                                                    wf_qkv[:, 2 * D:], start=True, stop=True)
                        last.then_inc(g["v_rows"], 1)
                    if has(5):
                        if not has(1):
                            pe.wait_ge(g["zt"], ob + i)
                        after(pe, g["logit"], o + i - 5)
                        for t in range(2):
                            last = nc.tensor.matmul(GB[:, t * E:(t + 1) * E], zt[:, c1, 1, t * P:(t + 1) * P], wg[:, :],
                                                    start=True, stop=True)
                        last.then_inc(g["gate"], 1)
                    if has(3):
                        pe.wait_ge(g["p_t"], o + i - 2)
                        pe.wait_ge(g["v"], o + i - 2)
                        after(pe, g["att_t"], o + i - 3)
                        for t in range(2):
                            for h in range(HM):
                                last = nc.tensor.matmul(AV[DM * h:DM * (h + 1), t * P:(t + 1) * P],
                                                        v_r[:, c3, t, DM * h:DM * (h + 1)], p_t[:, c3, t, h, :],
                                                        start=True, stop=True)
                        last.then_inc(g["att"], 1)
                pipeline(pe, PAIRS, DEPTH, 3, body, FIRST)

            @on("scalar")
            def _(act):
                g = m_s

                def body(i, s, has, lap):
                    c1, c2, c3 = ((s - k) % 3 for k in (1, 2, 3))
                    if has(1) or has(5):
                        act.wait_ge(g["turned"], ob + i)
                        lo, hi = (0 if has(1) else 1), (2 if has(5) else 1)
                        nc.scalar.activation(zt[:, c1, lo:hi, :],
                                             TT[:, 256 * lo:256 * hi].rearrange("p (n t) -> p n t", n=hi - lo),
                                             ACT.Copy, bias=HAT).then_inc(g["zt"], 1)
                    if has(1):
                        act.wait_ge(g["qk"], o + i)
                        nc.scalar.activation(q_t[:, c1, :], QK[:, 0:256], ACT.Copy, scale=DM ** -0.5)
                        for h in range(HM):
                            rows = slice(DM * h, DM * (h + 1))
                            last = nc.scalar.activation(k_x[rows, c1, :, :, h, :].rearrange("p t q k -> p (t q) k"),
                                                        QK[rows, 256:512].rearrange("p (n k) -> p n k", k=32), ACT.Copy)
                        last.then_inc(g["kx"], 1)
                        act.wait_ge(g["v_rows"], o + i)
                        nc.scalar.activation(v_r[:, c1, :, 0:P], VB[:, 0:256].rearrange("p (t n) -> p t n", t=2),
                                             ACT.Copy).then_inc(g["v"], 1)
                    if has(2):
                        act.wait_ge(g["centred"], o + i - 1)
                        nc.scalar.activation(sc[:, c2, :, :, :], sc[:, c2, :, :, :], ACT.Exp).then_inc(g["exp"], 1)
                    if has(5):
                        act.wait_ge(g["gate"], o + i - 4)
                        nc.scalar.activation(logit[:, bass.ds(i * 2 - 10, 2), :],
                                             GB[:, 0:2 * E].rearrange("p (t e) -> p t e", t=2), ACT.Copy).then_inc(g["logit"], 1)
                    if has(3):
                        act.wait_ge(g["att"], o + i - 2)
                        nc.scalar.activation(att_t[:, c3, :], AV[:, 0:256], ACT.Copy).then_inc(g["att_t"], 1)
                pipeline(act, PAIRS, DEPTH, 3, body, FIRST)

            @on("vector")
            def _(dve):
                g = m_s

                def body(i, s, has, lap):
                    c, c2, c3, c4 = ((s - k) % 3 for k in (0, 2, 3, 4))
                    if has(0):
                        if isinstance(i, int):
                            for k in range(G_PARTS):
                                lo = k * PAIRS // G_PARTS
                                if i == lo or (i == FIRST - 1 and lo > i):
                                    dve.wait_ge(x_back[k], 16 * (n + 1))
                        bn([tile(xa, i * 2), tile(xa, i * 2 + 1)], c, 0, g["stats0"])
                    if has(4):
                        dve.wait_ge(g["wo"], o + i - 3)
                        bn([WO[:, 0:P], WO[:, P:2 * P]], c, 2, g["stats1"])
                    if has(3):
                        dve.wait_ge(g["exp"], o + i - 2)
                        p = sc[:, c3, :, :, :].rearrange("p t h k -> p (t h) k")
                        nc.vector.tensor_reduce(out=sums[:, c3, :], in_=p, axis=AX.X, op=ALU.add).then_inc(g["sum"], 1)
                        dve.wait_ge(g["sum"], o + i - 2)
                        nc.vector.reciprocal(inv[:, c3, :], sums[:, c3, :]).then_inc(g["inv"], 1)
                        dve.wait_ge(g["inv"], o + i - 2)
                        nc.vector.tensor_tensor(p, p, inv[:, c3, :].unsqueeze(2).to_broadcast([P, 2 * HM, 32]),
                                                ALU.mult).then_inc(g["prob"], 1)
                    if has(2):
                        q = sc[:, c2, :, :, :].rearrange("p t h k -> p (t h) k")
                        dve.wait_ge(g["s"], o + i - 1)
                        nc.vector.tensor_tensor(q, SB[:, 0:256].rearrange("p (n k) -> p n k", k=32),
                                                far[:, :].unsqueeze(1).to_broadcast([P, 2 * HM, 32]),
                                                ALU.add).then_inc(g["masked"], 1)
                        dve.wait_ge(g["masked"], o + i - 1)
                        nc.vector.tensor_reduce(out=mx[:, c2, :], in_=q, axis=AX.X, op=ALU.max).then_inc(g["max"], 1)
                        dve.wait_ge(g["max"], o + i - 1)
                        nc.vector.tensor_tensor(q, q, mx[:, c2, :].unsqueeze(2).to_broadcast([P, 2 * HM, 32]),
                                                ALU.subtract).then_inc(g["centred"], 1)
                    if has(3):
                        dve.wait_ge(g["prob"], o + i - 2)
                        for q in range(4):
                            rows = slice(32 * q, 32 * q + 32)
                            last = nc.vector.transpose(
                                p_t[rows, c3, :, :, 32 * q:32 * q + 32].rearrange("p t h k -> p (t h) k"),
                                sc[rows, c3, :, :, :].rearrange("p t h k -> p (t h) k"))
                        last.then_inc(g["p_t"], 1)
                    if has(0) or has(4):
                        dve.wait_ge(g["rstd"], ob + i + 1)
                    if has(4):
                        for t in range(2):
                            last = nc.vector.tensor_scalar(z1[:, (s - 4) % 3, t, :], WO[:, t * P:(t + 1) * P],
                                                           mean[:, c, 0, 2 + t:3 + t], rstd[:, c, 2 + t:3 + t],
                                                           ALU.subtract, ALU.mult)
                        last.then_inc(g["z1"], 1)
                    if has(0):
                        for t in range(2):
                            last = normalise(z0[:, c, t, :], tile(xa, i * 2 + t), c, t)
                        last.then_inc(g["z0"], 1)
                pipeline(dve, PAIRS, DEPTH, 3, body, FIRST)

            @on("gpsimd")
            def _(pool):
                g = m_s

                def body(i, s, has, lap):
                    made = [(g["stats0"], o + i + 1)] * has(0) + [(g["stats1"], o + i - 3)] * has(4)
                    roots(pool, s % 3, ob + i, 4, made, g["step"], g["rstd"])
                    if has(4):
                        pool.wait_ge(g["z1"], o + i - 3)
                        nc.gpsimd.tensor_copy(both(z1_all, i - 4), z1[:, (s - 4) % 3, :, :]).then_inc(g["kept"], 1)
                pipeline(pool, PAIRS, DEPTH - 1, 3, body, FIRST)

        r_step, counted, offsets, placed, owned = (sem("r_" + k) for k in (
            "step", "counted", "offsets", "placed", "owned"))
        R_STEPS = 18

        def routing(n):
            RB = bank[7]

            @on("tensor")
            def _(pe):
                pe.wait_ge(counted, n + 1)
                nc.tensor.matmul(RB[:, 0:E], lower[:, :], cnt[:, :], start=True, stop=True)
                nc.tensor.matmul(RB[:, E:2 * E], ones[:, :], cnt[:, :], start=True, stop=True).then_inc(offsets, 1)

            @on("vector")
            def _(dve):
                made = [n * R_STEPS]

                def link(instruction):
                    made[0] += 1
                    instruction.then_inc(r_step, 1)
                    dve.wait_ge(r_step, made[0])

                def over_t(x):
                    return x.unsqueeze(2).to_broadcast([P, E, NT])

                dve.wait_ge(m_s["logit"], (n + 1) * PAIRS)
                link(nc.vector.tensor_reduce(out=best[:, :], in_=logit[:, :, :], axis=AX.X, op=ALU.max))
                link(nc.vector.tensor_tensor(seen[:, :, :], logit[:, :, :], best.unsqueeze(2).to_broadcast([P, NT, E]),
                                             ALU.is_ge))
                link(nc.vector.tensor_tensor(seen[:, :, :], seen[:, :, :], rank_w[:, :].unsqueeze(1).to_broadcast([P, NT, E]),
                                             ALU.mult))
                link(nc.vector.tensor_reduce(out=best[:, :], in_=seen[:, :, :], axis=AX.X, op=ALU.max))
                link(nc.vector.tensor_tensor(hot[:, :, :], over_t(rank_w[:, :]), best.unsqueeze(1).to_broadcast([P, E, NT]),
                                             ALU.is_equal))
                nc.vector.tensor_reduce(out=cnt[:, :], in_=hot[:, :, :], axis=AX.X, op=ALU.add).then_inc(counted, 1)
                nc.vector.tensor_tensor_scan(hot_inc.rearrange("p e t -> p (e t)"), resets[:, :],
                                             hot.rearrange("p e t -> p (e t)"), 0.0, ALU.mult, ALU.add)
                dve.wait_ge(offsets, n + 1)
                link(nc.vector.tensor_copy(tot[:, :], RB[:, 0:2 * E]))
                before, total = tot[:, 0:E], tot[:, E:2 * E]
                link(nc.vector.tensor_tensor(over[:, :, :], over_t(total), steps[:, :].unsqueeze(1).to_broadcast([P, E, NT]),
                                             ALU.is_gt))
                link(nc.vector.tensor_reduce(out=n_tiles[:, :], in_=over[:, :, :], axis=AX.X, op=ALU.add))
                link(nc.vector.tensor_tensor(ends_m[:, :, :], upto[:, :, :], n_tiles[:, :].unsqueeze(1).to_broadcast([P, E, E]),
                                             ALU.mult))
                link(nc.vector.tensor_reduce(out=ends[:, :], in_=ends_m[:, :, :], axis=AX.X, op=ALU.add))
                link(nc.vector.tensor_tensor(base[:, :], ends[:, :], n_tiles[:, :], ALU.subtract))
                link(nc.vector.scalar_tensor_tensor(out=base[:, :], in0=base[:, :], scalar=float(P), in1=before,
                                                    op0=ALU.mult, op1=ALU.add))
                link(nc.vector.tensor_scalar_add(base[:, :], base[:, :], -1.0))
                link(nc.vector.tensor_tensor(place[:, :, :], hot_inc[:, :, :], over_t(base[:, :]), ALU.add))
                link(nc.vector.tensor_tensor(place[:, :, :], place[:, :, :], hot[:, :, :], ALU.mult))
                link(nc.vector.tensor_reduce(out=pos_f[:, :], in_=place.rearrange("p e t -> p t e"), axis=AX.X, op=ALU.add))
                nc.vector.tensor_copy(pos[:, :], pos_f[:, :]).then_inc(placed, 1)
                link(nc.vector.tensor_tensor(owner_m[:, :, :], tile_no[:, :].unsqueeze(2).to_broadcast([P, ET, E]),
                                             ends[:, :].unsqueeze(1).to_broadcast([P, ET, E]), ALU.is_ge))
                link(nc.vector.tensor_reduce(out=owner_f[:, :], in_=owner_m[:, :, :], axis=AX.X, op=ALU.add))
                nc.vector.tensor_scalar_min(owner[:, :], owner_f[:, :], float(E - 1)).then_inc(owned, 1)
                assert made[0] == (n + 1) * R_STEPS, made

        e_s = {k: sem("e_" + k) for k in (
            "scattered", "turned", "zt", "w1", "w2", "hid_a", "hid_b", "relu_a", "relu_b", "v", "stats", "agg", "var",
            "rstd", "tmp", "y")}
        loaded = [sem(f"e_loaded{k}") for k in range(3)]
        stored = [sem(f"e_stored{k}") for k in range(3)]
        back = [sem(f"e_back{k}") for k in range(NT // 4)]

        def experts(n):
            o = n * ET
            laps = 16 * n * (ET // 3)
            DEPTH, FIRST = 5, 6
            TB, HA_, HB_ = bank[0], bank[1], bank[2]
            VB = [bank[3], bank[4], bank[5]]

            @on("gpsimd")
            def _(pool):
                g = e_s
                pool.wait_ge(m_s["kept"], (n + 1) * PAIRS)
                pool.wait_ge(placed, n + 1)
                if n == 0:
                    pool.wait_ge(zeros_out, ZEROS)
                for t in range(NT):
                    nc.gpsimd.indirect_dma_start(
                        sorted_dram[n][:, :], bass.IndirectOffsetOnAxis(ap=pos[:, t:t + 1], axis=0),
                        z1_all[:, t, :], None).then_inc(g["scattered"], 16)

                def body(i, s, has, lap):
                    if has(3):
                        pool.wait_ge(g["var"], o + i - 2)
                        nc.gpsimd.tensor_tensor(rstd[:, s % 3, 0:1], var_e[:, s % 3, :], half_neg[:, 0:1],
                                                ALU.pow).then_inc(g["rstd"], 1)
                pipeline(pool, ET, DEPTH - 1, 3, body, FIRST)
                for k in range(3):
                    pool.wait_ge(stored[k], laps + 16 * (ET // 3))
                for t in range(NT):
                    nc.gpsimd.indirect_dma_start(
                        z1_all[:, t, :], None, moved_dram[n][:, :],
                        bass.IndirectOffsetOnAxis(ap=pos[:, t:t + 1], axis=0)).then_inc(back[t // 4], 16)

            @on("sync")
            def _(sp):
                g = e_s
                sp.wait_ge(g["scattered"], (n + 1) * 16 * NT)

                def body(i, s, has, lap):
                    if has(0):
                        after(sp, g["turned"], o + i - 2)
                        sp.dma_start(zs[:, s % 3, :], sorted_dram[n][bass.ds(i * P, P), :]).then_inc(loaded[s % 3], 16)
                    if has(6):
                        sp.wait_ge(g["y"], o + i - 5)
                        sp.dma_start(moved_dram[n][bass.ds(i * P - 6 * P, P), :], xout[:, s % 3, 0, :])\
                            .then_inc(stored[s % 3], 16)
                pipeline(sp, ET, DEPTH + 2, 3, body, FIRST)

            @on("tensor")
            def _(pe):
                g = e_s

                def body(i, s, has, lap):
                    c, c1, c2 = s % 3, (s - 1) % 3, (s - 2) % 3
                    if has(0):
                        pe.wait_ge(loaded[c], lap(0) * 16 + (laps + 16))
                        after(pe, g["zt"], o + i)
                        nc.tensor.transpose(TB[:, 0:P], zs[:, c, :], ident[:, :]).then_inc(g["turned"], 1)
                    if has(1):
                        pe.wait_ge(g["zt"], o + i)
                        pe.wait_ge(g["w1"], o + i)
                        for m in range(FC):
                            if m == 0:
                                after(pe, g["relu_a"], o + i - 1)
                            if m == 2:
                                after(pe, g["relu_b"], o + i - 1)
                            to = HA_ if m < 2 else HB_
                            last = nc.tensor.matmul(to[:, (m % 2) * P:(m % 2 + 1) * P], we_t[:, c1, m * P:(m + 1) * P],
                                                    zt[:, c1, 0, 0:P], start=True, stop=True)
                            if m == 1:
                                last.then_inc(g["hid_a"], 1)
                        last.then_inc(g["hid_b"], 1)
                    if has(2):
                        pe.wait_ge(g["relu_a"], o + i - 1)
                        pe.wait_ge(g["relu_b"], o + i - 1)
                        pe.wait_ge(g["w2"], o + i - 1)
                        after(pe, g["tmp"], o + i - 4)
                        for m in range(FC):
                            nc.tensor.matmul(VB[c2][:, 0:P], hid_e[:, c2, m, :], we_t[:, c2, F + m * P:F + (m + 1) * P],
                                             start=(m == 0), stop=False)
                        nc.tensor.matmul(VB[c2][:, 0:P], zt[:, c2, 0, 0:P], we_t[:, c2, 2 * F:], start=False,
                                         stop=True).then_inc(g["v"], 1)
                pipeline(pe, ET, DEPTH - 2, 3, body, FIRST)

            @on("scalar")
            def _(act):
                g = e_s

                def body(i, s, has, lap):
                    c, c1 = s % 3, (s - 1) % 3
                    if has(0):
                        act.wait_ge(g["turned"], o + i + 1)
                        nc.scalar.activation(zt[:, c, 0, 0:P], TB[:, 0:P], ACT.Copy, bias=HAT).then_inc(g["zt"], 1)
                    if has(1):
                        act.wait_ge(g["hid_a"], o + i)
                        nc.scalar.activation(hid_e[:, c1, 0:2, :], HA_[:, 0:256].rearrange("p (m t) -> p m t", m=2),
                                             ACT.Relu).then_inc(g["relu_a"], 1)
                    if has(0):
                        after(act, g["hid_b"], o + i - 2)
                        e = act.value_load(owner[0:1, bass.ds(i, 1)], min_val=0, max_val=E - 1)
                        nc.scalar.activation(we_t[:, c, 0:F], we[:, bass.ds(e, 1), 0:F].rearrange("p a n -> p (a n)"),
                                             ACT.Copy).then_inc(g["w1"], 1)
                act.wait_ge(owned, n + 1)
                pipeline(act, ET, 2, 3, body, FIRST)

            @on("vector")
            def _(dve):
                g = e_s

                def body(i, s, has, lap):
                    c, c1 = s % 3, (s - 1) % 3
                    if has(3):
                        dve.wait_ge(g["v"], o + i - 2)
                        nc.vector.bn_stats(stats[:, c, 0, :], VB[c][:, 0:P]).then_inc(g["stats"], 1)
                        dve.wait_ge(g["stats"], o + i - 2)
                    if has(1):
                        dve.wait_ge(g["hid_b"], o + i)
                        nc.vector.tensor_scalar_max(hid_e[:, c1, 2:4, :], HB_[:, 0:256].rearrange("p (m t) -> p m t", m=2),
                                                    0.0).then_inc(g["relu_b"], 1)
                    if has(3):
                        nc.vector.bn_aggr(mv[:, c, :], stats[:, c, 0, :]).then_inc(g["agg"], 1)
                    if has(4):
                        dve.wait_ge(g["rstd"], o + i - 3)
                        nc.vector.scalar_tensor_tensor(out=tmp[:, c1, 0, :], in0=VB[c1][:, 0:P], scalar=mv[:, c1, 0:1],
                                                       in1=g2f[:, :], op0=ALU.subtract, op1=ALU.mult).then_inc(g["tmp"], 1)
                    if has(3):
                        dve.wait_ge(g["agg"], o + i - 2)
                        nc.vector.tensor_scalar_add(var_e[:, c, :], mv[:, c, 1:2], EPS).then_inc(g["var"], 1)
                    if has(4):
                        dve.wait_ge(g["tmp"], o + i - 3)
                        after(dve, stored[c1], lap(4) * 16 + laps)
                        nc.vector.scalar_tensor_tensor(out=xout[:, c1, 0, :], in0=tmp[:, c1, 0, :],
                                                       scalar=rstd[:, c1, 0:1], in1=b2f[:, :], op0=ALU.mult,
                                                       op1=ALU.add).then_inc(g["y"], 1)
                    if has(0):
                        after(dve, g["v"], o + i - 2)
                        e = dve.value_load(owner[0:1, bass.ds(i, 1)], min_val=0, max_val=E - 1)
                        nc.vector.tensor_copy(we_t[:, c, F:], we[:, bass.ds(e, 1), F:].rearrange("p a n -> p (a n)"))\
                            .then_inc(g["w2"], 1)
                dve.wait_ge(owned, n + 1)
                pipeline(dve, ET, DEPTH, 3, body, FIRST)

        summed, f_stored = sem("f_summed"), sem("f_stored")

        def finish(n, store):
            @on("vector")
            def _(dve):
                for k in range(NT // 4):
                    four = slice(4 * k, 4 * k + 4)
                    dve.wait_ge(back[k], 64 * (n + 1))
                    nc.vector.tensor_tensor(xa[:, four, :], xa[:, four, :], z1_all[:, four, :], ALU.add).then_inc(summed, 1)

            @on("sync")
            def _(sp):
                for k in range(NT // 4):
                    sp.wait_ge(summed, n * (NT // 4) + k + 1)
                    store(sp, k, f_stored)

        def to_x2(sp, k, signal):
            four = slice(4 * k, 4 * k + 4)
            sp.dma_start(x2_dram[:, :].rearrange("(t p) d -> p t d", p=P)[:, four, :], xa[:, four, :]).then_inc(signal, 16)

        def to_out(sp, k, signal):
            for t in range(4 * k, 4 * k + 4):
                sp.dma_start(out[:, 8 * t:8 * t + 8, :].rearrange("s b d -> b s d"), xa[:, t, :]).then_inc(signal, 16)

        def block_b():
            b_s = {k: sem("b_" + k) for k in (
                "stats0", "step", "rstd", "z0", "z", "turned", "zt", "gram", "gram_kept", "u", "u_a", "u_b", "m", "m_kept",
                "out", "x3")}
            x_b = [sem(f"b_x_in{k}") for k in range(4)]
            b_stored = [sem(f"b_stored{k}") for k in range(3)]
            DEPTH, FIRST = 5, 7
            TB, MB, OB = bank[0], bank[1], bank[2]
            G_COLS = slice(256, 384)

            @on("sync")
            def _(sp):
                sp.wait_ge(f_stored, 16 * (NT // 4))
                rows = x2_dram[:, :].rearrange("(h p s) d -> p h s d", p=P, s=S)
                for k in range(4):
                    for h in range(2):
                        sp.dma_start(xa[:, 8 * k:8 * k + 8, :].rearrange("p (s h) d -> p h s d", h=2)[:, h, :, :],
                                     rows[:, h, 4 * k:4 * k + 4, :]).then_inc(x_b[k], 16)
                x3_rows = x3_dram[:, :].rearrange("(h p s) d -> p h s d", p=P, s=S)

                def body(i, s, has, lap):
                    if has(4):
                        sp.wait_ge(b_s["x3"], i - 3)
                        sp.dma_start(x3_rows[:, :, bass.ds(i - 4, 1), :].rearrange("p h a d -> p h (a d)"),
                                     xout[:, (s - 4) % 3, :, :]).then_inc(b_stored[(s - 4) % 3], 16)
                pipeline(sp, PAIRS, DEPTH, 3, body, FIRST)

            @on("gpsimd")
            def _(pool):
                g = b_s

                def body(i, s, has, lap):
                    roots(pool, s % 3, i, 2, [(g["stats0"], i + 1)], g["step"], g["rstd"])
                    pool.wait_ge(g["z0"], i + 1)
                    nc.gpsimd.tensor_tensor(z1[:, s % 3, :, :], z0[:, s % 3, :, :], hats[:, :, :], ALU.add).then_inc(g["z"], 1)
                pipeline(pool, PAIRS, 1, 3, body, FIRST)

            @on("tensor")
            def _(pe):
                g = b_s

                def body(i, s, has, lap):
                    c1, c2, c3 = ((s - k) % 3 for k in (1, 2, 3))
                    if has(4):
                        pe.wait_ge(g["m_kept"], i - 3)
                        after(pe, g["x3"], i - 4)
                        for t in range(2):
                            last = nc.tensor.matmul(OB[:, t * P:(t + 1) * P], zt[:, c1, 0, t * P:(t + 1) * P],
                                                    m_sb[:, c1, :], start=True, stop=True)
                        last.then_inc(g["out"], 1)
                    if has(1):
                        pe.wait_ge(g["z"], i)
                        after(pe, g["gram_kept"], i - 1)
                        for t in range(2):
                            last = nc.tensor.transpose(TB[:, t * P:(t + 1) * P], z1[:, c1, t, :], ident[:, :])
                        last.then_inc(g["turned"], 1)
                        pe.wait_ge(g["zt"], i)
                        for t in range(2):
                            last = nc.tensor.matmul(TB[:, G_COLS], z1[:, c1, t, :], z1[:, c1, t, :], start=(t == 0),
                                                    stop=(t == 1))
                        last.then_inc(g["gram"], 1)
                    if has(2):
                        pe.wait_ge(g["gram_kept"], i - 1)
                        after(pe, g["u_a"], i - 2)
                        after(pe, g["u_b"], i - 2)
                        for k in range(4):
                            last = nc.tensor.matmul(wide[:, 512 * k:512 * (k + 1)], gram[:, c2, :],
                                                    vo[:, 4 * k:4 * k + 4, :].rearrange("p h d -> p (h d)"),
                                                    start=True, stop=True)
                            if k == 1:
                                last.then_inc(g["u"], 1)
                        last.then_inc(g["u"], 1)
                    if has(3):
                        pe.wait_ge(g["u_a"], i - 2)
                        pe.wait_ge(g["u_b"], i - 2)
                        after(pe, g["m_kept"], i - 3)
                        for h in range(HB):
                            nc.tensor.matmul(MB[:, 0:P], qk_t[:, h, :], u_sb[:, c3, h * D:(h + 1) * D], start=(h == 0),
                                             stop=False)
                        nc.tensor.matmul(MB[:, 0:P], spread[:, :], row_bo, start=False, stop=True).then_inc(g["m"], 1)
                pipeline(pe, PAIRS, DEPTH, 3, body, FIRST)

            @on("scalar")
            def _(act):
                g = b_s

                def body(i, s, has, lap):
                    c1, c2, c3 = ((s - k) % 3 for k in (1, 2, 3))
                    if has(1):
                        act.wait_ge(g["turned"], i)
                        nc.scalar.activation(zt[:, c1, 0, :], TB[:, 0:256], ACT.Copy).then_inc(g["zt"], 1)
                        act.wait_ge(g["gram"], i)
                        nc.scalar.activation(gram[:, c1, :], TB[:, G_COLS], ACT.Copy).then_inc(g["gram_kept"], 1)
                    if has(2):
                        act.wait_ge(g["u"], i * 2 - 3)
                        nc.scalar.activation(u_sb[:, c2, 0:1024], wide[:, 0:1024], ACT.Copy).then_inc(g["u_a"], 1)
                    if has(3):
                        act.wait_ge(g["m"], i - 2)
                        nc.scalar.activation(m_sb[:, c3, :], MB[:, 0:P], ACT.Copy).then_inc(g["m_kept"], 1)
                pipeline(act, PAIRS, DEPTH - 1, 3, body, FIRST)

            @on("vector")
            def _(dve):
                g = b_s

                def body(i, s, has, lap):
                    c, c1, c2 = ((s - k) % 3 for k in (0, 1, 2))
                    if has(0):
                        if isinstance(i, int):
                            for k in range(4):
                                if i == 4 * k or (i == FIRST - 1 and 4 * k > i):
                                    dve.wait_ge(x_b[k], 32)
                        bn([tile(xa, i * 2), tile(xa, i * 2 + 1)], c, 0, g["stats0"])
                    if has(4):
                        dve.wait_ge(g["out"], i - 3)
                        after(dve, b_stored[c1], lap(4) * 16)
                        nc.vector.tensor_tensor(xout[:, c1, :, :], OB[:, 0:256].rearrange("p (t d) -> p t d", t=2),
                                                both(xa, i - 4), ALU.add).then_inc(g["x3"], 1)
                    if has(0):
                        dve.wait_ge(g["rstd"], i + 1)
                        for t in range(2):
                            last = normalise(z0[:, c, t, :], tile(xa, i * 2 + t), c, t)
                        last.then_inc(g["z0"], 1)
                    if has(2):
                        dve.wait_ge(g["u"], i * 2 - 2)
                        nc.vector.tensor_copy(u_sb[:, c2, 1024:2048], wide[:, 1024:2048]).then_inc(g["u_b"], 1)
                pipeline(dve, PAIRS, DEPTH, 3, body, FIRST)
            return [(b_stored[k], 16 * len(range(k, PAIRS, 3))) for k in range(3)]

        a_done = [(s_, 16 * (PAIRS // 2)) for s_ in a_stored]
        attention_block(0, x1_dram, a_done)
        routing(0)
        experts(0)
        finish(0, to_x2)
        x3_done = block_b()
        attention_block(1, x3_dram, x3_done)
        routing(1)
        experts(1)
        finish(1, to_out)

        @on("sync")
        def _(sp):
            sp.wait_ge(zeros_out, ZEROS)
            sp.wait_ge(f_stored, 16 * (NT // 4) + 16 * NT)

        block = ctx.enter_context(nc.Block())

        @block.sync
        def _(eng):
            for stage in programs["sync"]:
                stage(eng)

        @block.gpsimd
        def _(eng):
            for stage in programs["gpsimd"]:
                stage(eng)

        @block.scalar
        def _(eng):
            for stage in programs["scalar"]:
                stage(eng)

        @block.vector
        def _(eng):
            for stage in programs["vector"]:
                stage(eng)

        @block.tensor
        def _(eng):
            for stage in programs["tensor"]:
                stage(eng)


def kernel(**inputs):
    import concourse.bacc as bacc
    from concourse.bass_utils import run_bass_kernel_spmd

    nc = bacc.Bacc("TRN2", target_bir_lowering=False, num_devices=1)
    arrays, dram = {}, {}
    for name, value in inputs.items():
        arrays[name] = np.ascontiguousarray(value)
        dram[name] = nc.dram_tensor(name, arrays[name].shape, mybir.dt.from_np(arrays[name].dtype), kind="ExternalInput").ap()
    out = nc.dram_tensor("out", (S, B, D), F32, kind="ExternalOutput").ap()
    build(nc, dram, out)
    result = run_bass_kernel_spmd(nc, [arrays], core_ids=[0])
    return result.results[0]["out"]
```

```python
from contextlib import ExitStack

import numpy as np
import concourse.bass as bass
from concourse import mybir

F32 = mybir.dt.float32
I32 = mybir.dt.int32
U32 = mybir.dt.uint32
ALU = mybir.AluOpType
ACT = mybir.ActivationFunctionType
AX = mybir.AxisListType

P = 128
D = 128
S, B = 16, 256
T = S * B
NT = T // P
PAIRS = NT // 2
HA = 16
HM, DM = 4, 32
HB, DB = 16, 64
F = 512
FC = F // P
E = 8
ET = (T + E * (P - 1)) // P
EW = F + F + D
ZS = 9
ROOM = T + 2 * P
PAY = 2 * D + 1
HAT = 0.125
ROW = 1.0 / (D * HAT)
EPS = 1e-5
FAR = -1e30


def pipeline(eng, n, depth, unroll, body, first):
    assert first >= depth - 1 and (n - first) % unroll == 0

    def peeled(i):
        body(i, i, lambda k: 0 <= i - k < n, lambda k, slots=unroll: (i - k) // slots)
    for i in range(first):
        peeled(i)
    if n > first:
        with eng.Fori(0, (n - first) // unroll) as j:
            for u in range(first, first + unroll):
                body(j * unroll + u, u, lambda k: True,
                     lambda k, slots=unroll: j * (unroll // slots) + (u - k) // slots)
    for i in range(n, n + depth - 1):
        peeled(i)


def after(eng, sem, count):
    if not (isinstance(count, int) and count <= 0):
        eng.wait_ge(sem, count)


def build(nc, A, out):
    ctx = ExitStack()
    with ctx:
        def sb(name, shape, dt=F32):
            return ctx.enter_context(nc.sbuf_tensor(name, shape, dt))

        def sem(name):
            return ctx.enter_context(nc.semaphore(name))

        bank = [ctx.enter_context(nc.psum_tensor(f"bank{b}", [P, 512], F32)) for b in range(4)]
        wide = ctx.enter_context(nc.psum_tensor("wide", [P, 2048], F32))
        bank += [wide[:, 512 * b:512 * (b + 1)] for b in range(4)]

        x1_dram = nc.dram_tensor("x1_dram", [T, D], F32)
        x2_dram = nc.dram_tensor("x2_dram", [T, D], F32)
        x3_dram = nc.dram_tensor("x3_dram", [T, D], F32)
        sorted_dram = [nc.dram_tensor(f"sorted{n}_dram", [P + E * ROOM, PAY], F32) for n in range(2)]

        ident = sb("ident", [P, P])
        zero = sb("zero", [P, PAY - D])
        spread = sb("spread", [1, P])
        half_neg = sb("half_neg", [P, 8])
        minus_half = sb("minus_half", [P, 2, 6])
        minus1 = sb("minus1", [P, 1])
        hats = sb("hats", [P, 2, D])
        blk8 = sb("blk8", [P, P])
        far = sb("far", [P, 32])
        lower = sb("lower", [P, P])
        ones = sb("ones", [P, P])
        rank_w = sb("rank_w", [P, E])
        upto = sb("upto", [P, E, E])
        steps = sb("steps", [P, NT])
        tile_no = sb("tile_no", [P, ET])
        rooms = sb("rooms", [P, E])
        rooms_row = sb("rooms_row", [P, E])
        reached = sb("reached", [P, 7])
        b_low = sb("b_low", [P, 1])
        token_f = sb("token_f", [P, NT])
        token = sb("token", [P, NT], U32)

        wa_qkv = sb("wa_qkv", [P, 3 * D])
        wa_o = sb("wa_o", [P, D])
        ra0 = sb("ra0", [P, D])
        wa1 = sb("wa1", [P, F])
        wa2 = sb("wa2", [P, FC, D])
        ra1 = sb("ra1", [P, D])
        col = sb("col", [P, 4])
        col16 = sb("col16", [P, 4])
        g2a, b2a = sb("g2a", [P, D]), sb("b2a", [P, D])
        centre = sb("centre", [P, P])
        cols_b = sb("cols_b", [P, 3, HB // 2])
        bo = sb("bo", [P, D])
        g2f, b2f = sb("g2f", [P, D]), sb("b2f", [P, D])
        wg_raw = sb("wg_raw", [E, D])
        wf_qkv = sb("wf_qkv", [P, 3 * D])
        wf_o = sb("wf_o", [P, D])
        wg_t = sb("wg_t", [P, E])
        wg = sb("wg", [P, E])
        rf0 = sb("rf0", [P, D])
        we = sb("we", [P, E, EW])
        ident4 = ident[:, :].unsqueeze(1).to_broadcast([P, 4, P])
        wb_o = sb("wb_o", [P, HB // 2, D])
        qk_t = sb("qk_t", [P, HB, D])
        vo = sb("vo", [P, HB, D])

        xa = sb("xa", [P, NT, D])
        stats = sb("stats", [P, 3, 6, 6])
        both_m = sb("both_m", [P, 3, 2, 6])
        mean = sb("mean", [P, 3, 2, 6])
        spread_m = sb("spread_m", [P, 3, 2, 6])
        rstd = sb("rstd", [P, 3, 6])
        shift = sb("shift", [P, 3, 2])
        z0 = sb("z0", [P, 3, 2, D])
        z1 = sb("z1", [P, 3, 2, D])
        zt = sb("zt", [P, 3, 2, 2 * P])
        q_t = sb("q_t", [P, 3, 2 * P])
        v_r = sb("v_r", [P, 3, 2, P + 2])
        att_t = sb("att_t", [P, 3, 2 * P])
        tmp = sb("tmp", [P, 3, 2, D])
        xout = sb("xout", [P, 3, 2, D])
        sc = sb("sc", [P, 3, 2, HM, 32])
        mx = sb("mx", [P, 3, 2 * HM])
        sums = sb("sums", [P, 3, 2 * HM])
        inv = sb("inv", [P, 3, 2 * HM])
        best = sb("best", [P, 2])
        seen = sb("seen", [P, 2, E])
        hot = sb("hot", [P, 3, 2, E])
        gone = sb("gone", [P, 3, 2, E])
        place = sb("place", [P, 2, E])
        pos = sb("pos", [P, 3, 2], U32)
        room_end = sb("room_end", [P, E])
        pad_at = sb("pad_at", [P, E], I32)
        n_tiles = sb("n_tiles", [P, E])
        ends = sb("ends", [P, E])
        skip = sb("skip", [P, E])
        beyond = sb("beyond", [P, ET])
        tile_of = sb("tile_of", [P, ET])
        owner_f = sb("owner_f", [P, ET])
        owner = sb("owner", [P, ET], I32)
        first_f = sb("first_f", [P, ET])
        first_row = sb("first_row", [P, ET], I32)
        dest = sb("dest", [P, 3, 1], U32)
        var_e = sb("var_e", [P, 3, 1])
        mv = sb("mv", [P, 3, 2])
        gram = sb("gram", [P, 3, P])
        m_sb = sb("m_sb", [P, 3, D])

        early = sb("early", [P, 6144])
        late = sb("late", [P, 6144])
        rows_f = sb("rows_f", [P, 2048])
        rows_e = sb("rows_e", [P, E * F])
        hid_f = sb("hid_f", [P, 2048])

        def parts(whole, *shapes):
            at, cut = 0, []
            for shape in shapes:
                size = int(np.prod(shape))
                part = whole[:, at:at + size]
                names = "abcdef"[:len(shape)]
                if len(shape) > 1:
                    part = part.rearrange(f"p ({' '.join(names)}) -> p {' '.join(names)}",
                                          **dict(zip(names[1:], shape[1:])))
                cut.append(part)
                at += size
            assert at <= whole.shape[1], at
            return cut

        HALF = 3 * HB * DB
        wa_raw, wa1_raw, wf_raw, wf_t, wfo_raw, row_a2, fold_a, fold_f = parts(
            early[:, HALF:], (3 * D,), (F,), (3, D), (3 * D,), (D,), (D + F + D,), (P,), (P,))
        bias_b, = parts(late, (P,))
        wb_raw, wb_t = parts(early, (3, HB * DB), (3, HB // 2, D))
        bias_b2, row_f, row_a = parts(rows_f, (E * D,), (4 * D,), (3 * D,))
        bias_b1 = rows_e
        row_f, row_a, row_a2 = row_f[0:1], row_a[0:1], row_a2[0:1]
        k_r, exp_q, exp_k, kv, den, xres = parts(
            early[:, 0:HALF], (2, 2, P), (2, 2 * P), (2, 2, P), (2, 2, P), (2, 2 * P), (2, 2, D))
        hid, = parts(hid_f, (2, FC, 2 * P))
        k_x, p_t = parts(early, (3, 2, 4, HM, 32), (3, 2, HM, P))
        we_t, over, owner_m, skip_m, ends_m = parts(late, (3, EW), (E, NT), (ET, E), (ET, E), (E, E))
        pay, zs = parts(rows_e, (3, 2, PAY), (ZS, PAY))
        hid_e, = parts(hid_f, (3, FC, P))
        u_sb, = parts(late, (3, HB * D))

        blk16 = att_t[:, 0, 0:P]

        consts_made = sem("consts_made")
        const_step = sem("const_step")
        stats_init = sem("stats_init")

        programs = {"sync": [], "gpsimd": [], "scalar": [], "vector": [], "tensor": []}

        def on(engine):
            def add(f):
                programs[engine].append(f)
                return f
            return add

        @on("gpsimd")
        def _(pool):
            nc.gpsimd.memset(zero[:, :], 0.0).then_inc(const_step, 1)
            nc.gpsimd.memset(ones[:, :], 1.0).then_inc(const_step, 1)
            nc.gpsimd.memset(spread[:, :], ROW).then_inc(const_step, 1)
            nc.gpsimd.memset(half_neg[:, :], -0.5).then_inc(const_step, 1)
            nc.gpsimd.memset(hats[:, :, :], HAT)
            nc.gpsimd.memset(minus1[:, :], -1.0)
            nc.gpsimd.memset(minus_half[:, :, :], -0.5)
            nc.gpsimd.memset(stats[:, :, :, :], 1.0).then_inc(stats_init, 1)
            nc.gpsimd.iota(rooms[:, :], [[ROOM, E]], base=P, channel_multiplier=0,
                           allow_small_or_imprecise_dtypes=True).then_inc(const_step, 1)
            pool.wait_ge(const_step, 5)

            def select(out_, in_, pattern, base, mult, op, fill):
                return nc.gpsimd.affine_select(out=out_, in_=in_, compare_op=op, fill=fill, base=base,
                                               pattern=pattern, channel_multiplier=mult)
            select(ident[:, :], zero[:, 0:P], [[-1, P]], 0, 1, ALU.not_equal, 1.0).then_inc(const_step, 1)
            select(lower[:, :], ones[:, :], [[1, P]], 0, -1, ALU.is_gt, 0.0).then_inc(const_step, 1)
            select(blk8[:, :], ones[:, :], [[-8, HA], [0, 8]], 0, 1, ALU.is_ge, 0.0).then_inc(const_step, 1)
            pool.wait_ge(const_step, 8)
            select(blk8[:, :], blk8[:, :], [[8, HA], [0, 8]], 7, -1, ALU.is_ge, 0.0).then_inc(const_step, 1)
            nc.gpsimd.tensor_scalar(centre[:, :], ident[:, :], 1.0, -1.0 / D, ALU.mult, ALU.add).then_inc(const_step, 1)
            nc.gpsimd.iota(rank_w[:, :], [[-1, E]], base=E, channel_multiplier=0,
                           allow_small_or_imprecise_dtypes=True).then_inc(const_step, 1)
            nc.gpsimd.iota(steps[:, :], [[P, NT]], base=0, channel_multiplier=0,
                           allow_small_or_imprecise_dtypes=True).then_inc(const_step, 1)
            nc.gpsimd.iota(tile_no[:, :], [[1, ET]], base=0, channel_multiplier=0,
                           allow_small_or_imprecise_dtypes=True).then_inc(const_step, 1)
            select(upto[:, :, :], ones[:, 0:E * E].rearrange("p (e f) -> p e f", e=E), [[1, E], [-1, E]], 0, 0,
                   ALU.is_ge, 0.0).then_inc(const_step, 1)
            select(rooms_row[:, :], rooms[:, :], [[0, E]], 0, -1, ALU.is_ge, 0.0).then_inc(const_step, 1)
            select(blk16, ones[:, :], [[-16, 8], [0, 16]], 0, 1, ALU.is_ge, 0.0).then_inc(const_step, 1)
            pool.wait_ge(const_step, 16)
            select(blk16, blk16, [[16, 8], [0, 16]], 15, -1, ALU.is_ge, 0.0).then_inc(const_step, 1)
            select(reached[:, :], ones[:, 0:7], [[-16, 7]], -16, 1, ALU.is_ge, 0.0).then_inc(const_step, 1)
            nc.gpsimd.iota(token_f[:, :], [[P // 16, NT]], base=0, channel_multiplier=B,
                           allow_small_or_imprecise_dtypes=True).then_inc(const_step, 1)
            pool.wait_ge(const_step, 19)
            nc.gpsimd.memset(z0[0:1, 0, 0, 0:1], 0.0).then_inc(consts_made, 1)

        w_q_in = sem("w_q_in")
        w_a_in = sem("w_a_in")
        w_o_in = sem("w_o_in")
        firsts_out = sem("firsts_out")

        def row(v):
            return v.rearrange("(a n) -> a n", a=1)

        def column(v):
            return v.rearrange("(n a) -> n a", a=1)

        X_PARTS = ((0, 2), (2, 8), (8, 16), (16, 24), (24, 32))
        x_in = [sem(f"x_in{n}") for n in range(len(X_PARTS))]
        a = {n[10:]: A[n] for n in A if n.startswith("L0_attn_a_")}
        f = {n[7:]: A[n] for n in A if n.startswith("L0_ffn_")}
        b = {n[10:]: A[n] for n in A if n.startswith("L0_attn_b_")}
        loads_q = [(wa_raw[:, 0:D], a["Wq"]), (wa_raw[:, D:2 * D], a["Wk"]), (wa_raw[:, 2 * D:], a["Wv"]),
                   (row_a[:, 0:D], row(a["bq"])), (row_a[:, D:2 * D], row(a["bk"])), (row_a[:, 2 * D:], row(a["bv"]))]
        loads_a = [(row_a2[:, 0:D], row(a["bo"])), (row_a2[:, D:D + F], row(a["b1"])), (row_a2[:, D + F:], row(a["b2"])),
                   (wa_o[:, :], a["Wo"]), (wa1_raw[:, :], a["W1"]),
                   (wa2[:, :, :], a["W2"].rearrange("(c p) d -> p c d", p=P)),
                   (col[:, 0:1], column(a["g1"])), (col[:, 1:2], column(a["beta1"])),
                   (col[:, 2:3], column(f["g1"])), (col[:, 3:4], column(f["be1"])),
                   (g2a[:, :], row(a["g2"]).to_broadcast([P, D])), (b2a[:, :], row(a["beta2"]).to_broadcast([P, D]))]
        loads_o = [(wf_raw[:, :, :], f["Wqkv"].rearrange("(c p) d -> p c d", p=P)), (wfo_raw[:, :], f["Wo"]),
                   (wg_raw[:, :], f["Wg"]), (row_f[:, 0:3 * D], row(f["bqkv"])), (row_f[:, 3 * D:], row(f["bo"])),
                   (bias_b1[:, :], f["b1"].rearrange("(a e) n -> a (e n)", a=1).to_broadcast([P, E * F])),
                   (bias_b2[:, :], f["b2"].rearrange("(a e) n -> a (e n)", a=1).to_broadcast([P, E * D])),
                   (g2f[:, :], row(f["g2"]).to_broadcast([P, D])), (b2f[:, :], row(f["be2"]).to_broadcast([P, D]))]
        loads_o += [(we[:, e, 0:F], f["W1"][e]) for e in range(E)]
        loads_o += [(we[:, e, F:2 * F].rearrange("p (c d) -> p c d", c=FC),
                     f["W2"][e].rearrange("(c p) d -> p c d", p=P)) for e in range(E)]
        loads_o += [(bias_b[8 * m:8 * m + 8, :], b[v].rearrange("(c p) -> c p", p=P))
                    for m, v in enumerate(("bq", "bk", "bv"))]
        loads_o += [(bo[:, :], row(b["bo"]).to_broadcast([P, D])),
                    (wb_o[:, :, :], b["Wo"].rearrange("(c p) d -> p c d", p=P))]

        @on("sync")
        def _(sp):
            xs = a["x"].rearrange("s (h p) d -> p (s h) d", p=P)
            for n, (lo, hi) in enumerate(X_PARTS):
                sp.dma_start(xa[:, lo:hi, :], xs[:, lo:hi, :]).then_inc(x_in[n], 16)
                if n == 0:
                    for dst, src in loads_q:
                        sp.dma_start(dst, src).then_inc(w_q_in, 16)
                    for dst, src in loads_a:
                        sp.dma_start(dst, src).then_inc(w_a_in, 16)
            for dst, src in loads_o:
                sp.dma_start(dst, src).then_inc(w_o_in, 16)
            sp.wait_ge(consts_made, 1)
            for d in sorted_dram:
                for lo, hi in ((0, D), (D, PAY)):
                    sp.dma_start(d[0:E * ROOM, :].rearrange("(e r) d -> e r d", e=E)[:, 0:1, lo:hi].rearrange("e a d -> (e a) d"),
                                 zero[0:E, 0:hi - lo]).then_inc(firsts_out, 16)

        rows_made = sem("rows_made")
        fold_step = sem("fold_step")
        folds_made = sem("folds_made")
        hat_done = sem("hat_done")
        hat_kept = sem("hat_kept")
        ones_col = sem("ones_col")
        tokens_made = sem("tokens_made")
        k_cleared, p_cleared = sem("k_cleared"), sem("p_cleared")

        @on("vector")
        def _(dve):
            dve.wait_ge(w_q_in, 16 * len(loads_q))
            nc.vector.tensor_scalar_add(row_a[0:1, 0:2 * D], row_a[0:1, 0:2 * D], 1.0).then_inc(rows_made, 1)
            dve.wait_ge(w_a_in, 16 * len(loads_a))
            dve.wait_ge(consts_made, 1)
            nc.vector.tensor_scalar_mul(col16[:, :], col[:, :], ROW).then_inc(fold_step, 1)
            dve.wait_ge(fold_step, 1)
            nc.vector.tensor_scalar(fold_a[:, :], centre[:, :], col[:, 0:1], col16[:, 1:2], ALU.mult, ALU.add)
            nc.vector.tensor_scalar(fold_f[:, :], centre[:, :], col[:, 2:3], col16[:, 3:4], ALU.mult,
                                    ALU.add).then_inc(folds_made, 1)
            nc.vector.tensor_reduce(out=far[:, :], in_=blk16.rearrange("p (q c) -> p c q", q=4), axis=AX.X,
                                    op=ALU.add).then_inc(fold_step, 1)
            dve.wait_ge(fold_step, 2)
            nc.vector.tensor_scalar(far[:, :], far[:, :], -1.0, -FAR, ALU.add, ALU.mult).then_inc(fold_step, 1)
            nc.vector.memset(v_r[:, :, :, P:P + 1], 1.0).then_inc(ones_col, 1)
            nc.vector.tensor_reduce(out=b_low[:, :], in_=reached[:, :], axis=AX.X, op=ALU.add).then_inc(fold_step, 1)
            dve.wait_ge(fold_step, 4)
            nc.vector.tensor_scalar_mul(b_low[:, :], b_low[:, :], 1.0 - 16 * B).then_inc(fold_step, 1)
            dve.wait_ge(fold_step, 5)
            nc.vector.tensor_scalar(token[:, :], token_f[:, :], b_low[:, 0:1], None, ALU.add).then_inc(tokens_made, 1)

        HAT_BANK, HAT_BANK_B = (4, 5), (6, 7)

        def hat(width, lhsT, rhs, bias, dst, **kw):
            return dict(width=width, parts=[(0, width, [(lhsT, rhs)] + ([(spread[:, :], bias)] if bias is not None else []))],
                        dst=dst, **kw)

        hats_a = [hat(3 * D, centre[:, :], wa_raw[:, :], row_a[:, :], wa_qkv[:, :]),
                  hat(D, centre[:, :], ident[:, :], row_a2[:, 0:D], ra0[:, :]),
                  hat(F, fold_a[:, :], wa1_raw[:, :], row_a2[:, D:D + F], wa1[:, :]),
                  hat(D, fold_a[:, :], ident[:, :], row_a2[:, D + F:], ra1[:, :])]
        N_A = len(hats_a)
        turned = [dict(width=3 * D, turns=[(n * D, wf_raw[:, n, :], ident[:, :]) for n in range(3)], dst=wf_t[:, :]),
                  dict(width=D, turns=[(0, wfo_raw[:, :], ident[:, :])], dst=wf_o[:, :]),
                  dict(width=E, turns=[(0, wg_raw[:, :], ident[0:E, 0:E])], dst=wg_t[:, :])]
        hats_f = turned + [hat(3 * D, centre[:, :], wf_t[:, :], row_f[:, 0:3 * D], wf_qkv[:, :], after=N_A + 1),
                           hat(D, centre[:, :], ident[:, :], row_f[:, 3 * D:], rf0[:, :]),
                           hat(E, fold_f[:, :], wg_t[:, :], None, wg[:, :], after=N_A + 3)]
        hats_f += [hat(F, fold_f[:, :], we[:, e, 0:F], None, we[:, e, 0:F], rows=bias_b1[:, e * F:(e + 1) * F])
                   for e in range(E)]
        hats_f += [hat(4 * D, fold_f[:, :], ident4, None, we[:, e:e + 4, 2 * F:], rows=bias_b2[:, e * D:(e + 4) * D])
                   for e in (0, 4)]
        hats_f.append(dict(width=3 * HB // 2, turns=[(0, bias_b[0:24, :], ident[0:24, 0:24])], scale=ROW,
                           dst=cols_b[:, :, :].rearrange("p m c -> p (m c)")))
        hats_b = [dict(width=4 * P, dst=wb_t[:, m, c:c + 4, :], cols=cols_b[:, m, c:c + 4],
                        parts=[(n * P, P, [(wb_raw[:, m, (c + n) * P:(c + n + 1) * P], centre[:, :])])
                               for n in range(4)]) for m in range(3) for c in (0, 4)]
        N_T = N_A + len(hats_f) + len(hats_b)
        for h0 in (0, 1, 8, 9):
            lo = DB * (h0 % 2)
            hats_b.append(dict(width=4 * P, dst=qk_t[:, h0:h0 + 7:2, :], after=N_T,
                               parts=[(n * P, P, [(wb_t[lo:lo + DB, 1, h0 // 2 + n, :], wb_t[lo:lo + DB, 0, h0 // 2 + n, :])])
                                      for n in range(4)]))
        for h0 in (0, 1, 8, 9):
            lo = DB * (h0 % 2)
            hats_b.append(dict(width=4 * P, dst=vo[:, h0:h0 + 7:2, :], scale=DB ** -0.5,
                               parts=[(n * P, P, [(wb_t[lo:lo + DB, 2, h0 // 2 + n, :], wb_o[lo:lo + DB, h0 // 2 + n, :])])
                                      for n in range(4)]))
        N_F = N_A + len(hats_f)
        N_HATS = N_F + len(hats_b)
        hats_b1, hats_b2 = hats_b[:6], hats_b[6:]

        def hat_bank(n):
            return bank[(HAT_BANK if n < N_F else HAT_BANK_B)[n % 2]]

        def hat_products(pe, jobs, first):
            for n, job in enumerate(jobs, first):
                to = hat_bank(n)
                after(pe, hat_kept, max(n - 1, job.get("after", 0)))
                for at, lhsT, eye in job.get("turns", []):
                    last = nc.tensor.transpose(to[:, at:at + lhsT.shape[0]], lhsT, eye)
                for at, w, factors in job.get("parts", []):
                    for m, (lhsT, rhs) in enumerate(factors):
                        last = nc.tensor.matmul(to[:, at:at + w], lhsT, rhs, start=(m == 0), stop=(m == len(factors) - 1))
                last.then_inc(hat_done, 1)

        def with_bias(job):
            return "rows" in job or "cols" in job

        def hat_copies(eng, jobs, first, of_vector=False):
            for n, job in enumerate(jobs, first):
                if with_bias(job) != of_vector:
                    continue
                eng.wait_ge(hat_done, n + 1)
                after(eng, hat_kept, n)
                src = hat_bank(n)[:, 0:job["width"]]
                dst = job["dst"]

                def shaped(x):
                    return x.rearrange("p (n d) -> p n d", n=dst.shape[1]) if len(dst.shape) == 3 else x
                if "rows" in job:
                    copy = nc.vector.scalar_tensor_tensor(out=dst, in0=shaped(job["rows"]), scalar=ROW, in1=shaped(src),
                                                          op0=ALU.mult, op1=ALU.add)
                elif "cols" in job:
                    copy = nc.vector.tensor_tensor(dst, shaped(src), job["cols"].unsqueeze(2).to_broadcast([P, 4, P]),
                                                   ALU.add)
                else:
                    copy = nc.scalar.activation(dst, shaped(src), ACT.Copy, scale=job.get("scale", 1.0))
                copy.then_inc(hat_kept, 1)

        @on("tensor")
        def _(pe):
            pe.wait_ge(consts_made, 1)
            pe.wait_ge(w_q_in, 16 * len(loads_q))
            pe.wait_ge(rows_made, 1)
            hat_products(pe, hats_a[:1], 0)
            pe.wait_ge(w_a_in, 16 * len(loads_a))
            pe.wait_ge(folds_made, 1)
            hat_products(pe, hats_a[1:], 1)

        @on("scalar")
        def _(act):
            hat_copies(act, hats_a, 0)

        def tile(x, n):
            return x[:, bass.ds(n, 1), :].rearrange("p a d -> p (a d)")

        def both(x, n):
            return x[:, bass.ds(n * 2, 2), :]

        def bn(sources, slot, at, done):
            for n, x in enumerate(sources):
                last = nc.vector.bn_stats(stats[:, slot, at + n, :], x)
            last.then_inc(done, 1)

        def roots(pool, slot, body_no, lo, hi, made, step, rstd_made):
            st, w = stats[:, slot], slice(lo, hi)
            for sem_, count in made:
                pool.wait_ge(sem_, count)
            nc.gpsimd.tensor_tensor(both_m[:, slot, 0, w], st[:, w, 1], st[:, w, 4], ALU.add)
            nc.gpsimd.tensor_tensor(both_m[:, slot, 1, w], st[:, w, 1], st[:, w, 4], ALU.subtract)
            nc.gpsimd.tensor_tensor(spread_m[:, slot, 0, w], st[:, w, 2], st[:, w, 5], ALU.add).then_inc(step, 1)
            pool.wait_ge(step, body_no * 4 + 1)
            nc.gpsimd.tensor_tensor(mean[:, slot, :, w], both_m[:, slot, :, w], minus_half[:, :, w], ALU.mult)
            nc.gpsimd.tensor_scalar(spread_m[:, slot, 1, w], spread_m[:, slot, 0, w], 1.0 / D, EPS, ALU.mult,
                                    ALU.add).then_inc(step, 1)
            pool.wait_ge(step, body_no * 4 + 2)
            nc.gpsimd.tensor_tensor(spread_m[:, slot, 0, w], mean[:, slot, 1, w], mean[:, slot, 1, w],
                                    ALU.mult).then_inc(step, 1)
            pool.wait_ge(step, body_no * 4 + 3)
            nc.gpsimd.tensor_tensor(spread_m[:, slot, 0, w], spread_m[:, slot, 0, w], spread_m[:, slot, 1, w],
                                    ALU.add).then_inc(step, 1)
            pool.wait_ge(step, body_no * 4 + 4)
            nc.gpsimd.tensor_tensor(rstd[:, slot, w], spread_m[:, slot, 0, w], half_neg[:, w],
                                    ALU.pow).then_inc(rstd_made, 1)

        def normalise(dst, src, slot, at):
            return nc.vector.tensor_scalar(dst, src, mean[:, slot, 0, at:at + 1], rstd[:, slot, at:at + 1],
                                           ALU.add, ALU.mult)

        a_s = {n: sem("a_" + n) for n in (
            "stats0", "stats1", "stats2", "step", "step1", "rstd", "rstd1", "z0", "z1", "turned", "zt", "zt1", "kv_rows", "q_cols",
            "exp_q", "v", "phi", "sums", "masked", "att", "den", "inv", "att_t", "wo", "hid_a", "hid_b",
            "relu_a", "relu_b", "w2", "xres", "tmp", "x1")}
        a_stored = [sem(f"a_stored{n}") for n in range(2)]
        A_DEPTH, A_FIRST = 7, 8
        TT, QM, KV, ND, WO, W2B = bank[0], bank[1], bank[2], bank[3], bank[6], bank[7]
        WH = wide[:, 0:1024]

        @on("tensor")
        def _(pe):
            g = a_s
            pe.wait_ge(hat_kept, N_A)
            pe.wait_ge(ones_col, 1)

            def body(i, s, has, lap):
                c, l = s % 2, (s - 1) % 2
                if has(3):
                    pe.wait_ge(g["att_t"], i - 2)
                    after(pe, g["z1"], i - 3)
                    for t in range(2):
                        cut = slice(t * P, (t + 1) * P)
                        nc.tensor.matmul(WO[:, cut], att_t[:, l, cut], wa_o[:, :], start=True, stop=False)
                        last = nc.tensor.matmul(WO[:, cut], zt[:, l, 0, cut], ra0[:, :], start=False, stop=True)
                    last.then_inc(g["wo"], 1)
                if has(1) or has(4):
                    if has(2):
                        pe.wait_ge(g["zt"], i - 1)
                    if has(5):
                        pe.wait_ge(g["zt1"], i - 4)
                    if has(1):
                        pe.wait_ge(g["z0"], i)
                        for t in range(2):
                            last = nc.tensor.transpose(TT[:, t * P:(t + 1) * P], z0[:, l, t, :], ident[:, :])
                    if has(4):
                        pe.wait_ge(g["z1"], i - 3)
                        for t in range(2):
                            last = nc.tensor.transpose(TT[:, 256 + t * P:256 + (t + 1) * P], z1[:, l, t, :], ident[:, :])
                    last.then_inc(g["turned"], 1)
                if has(2):
                    pe.wait_ge(g["v"], i - 1)
                    pe.wait_ge(g["phi"], i - 1)
                    for t in range(2):
                        last = nc.tensor.matmul(QM[:, 256:256 + P + 1], k_r[:, c, t, :], v_r[:, c, t, 0:P + 1],
                                                start=(t == 0), stop=(t == 1))
                    last.then_inc(g["sums"], 1)
                if has(1):
                    pe.wait_ge(g["zt"], i)
                    for t in range(2):
                        last = nc.tensor.matmul(KV[:, t * 256:(t + 1) * 256], zt[:, l, 0, t * P:(t + 1) * P],
                                                wa_qkv[:, D:3 * D], start=True, stop=True)
                    last.then_inc(g["kv_rows"], 1)
                    if has(2):
                        pe.wait_ge(g["masked"], i - 1)
                    nc.tensor.matmul(QM[:, 0:256], wa_qkv[:, 0:D], zt[:, l, 0, :], start=True,
                                     stop=True).then_inc(g["q_cols"], 1)
                if has(2):
                    pe.wait_ge(g["masked"], i - 1)
                    after(pe, g["att_t"], i - 2)
                    nc.tensor.matmul(ND[:, 0:256], kv[:, c, 0, :], q_t[:, c, :], start=True, stop=True)
                    nc.tensor.matmul(ND[:, 256:512], kv[:, c, 1, :], q_t[:, c, :], start=True,
                                     stop=True).then_inc(g["att"], 1)
                if has(4):
                    pe.wait_ge(g["zt1"], i - 3)
                    for m in range(FC):
                        if m == 0:
                            after(pe, g["relu_a"], i - 4)
                        if m == 2:
                            after(pe, g["relu_b"], i - 4)
                        last = nc.tensor.matmul(WH[:, m * 256:(m + 1) * 256], wa1[:, m * P:(m + 1) * P],
                                                zt[:, l, 1, :], start=True, stop=True)
                        if m == 1:
                            last.then_inc(g["hid_a"], 1)
                    last.then_inc(g["hid_b"], 1)
                if has(5):
                    pe.wait_ge(g["relu_a"], i - 4)
                    pe.wait_ge(g["relu_b"], i - 4)
                    after(pe, g["tmp"], i - 5)
                    for t in range(2):
                        cut = slice(t * P, (t + 1) * P)
                        for m in range(FC):
                            nc.tensor.matmul(W2B[:, cut], hid[:, l, m, cut], wa2[:, m, :], start=(m == 0), stop=False)
                        last = nc.tensor.matmul(W2B[:, cut], zt[:, c, 1, cut], ra1[:, :], start=False, stop=True)
                    last.then_inc(g["w2"], 1)
            pipeline(pe, PAIRS, A_DEPTH, 2, body, A_FIRST)

        @on("scalar")
        def _(act):
            g = a_s

            def body(i, s, has, lap):
                c, l = s % 2, (s - 1) % 2
                if has(1) or has(4):
                    act.wait_ge(g["turned"], i)
                if has(1):
                    nc.scalar.activation(zt[:, l, 0, :], TT[:, 0:256], ACT.Copy, bias=HAT).then_inc(g["zt"], 1)
                if has(4):
                    nc.scalar.activation(zt[:, l, 1, :], TT[:, 256:512], ACT.Copy, bias=HAT).then_inc(g["zt1"], 1)
                if has(1):
                    act.wait_ge(g["kv_rows"], i)
                    rows = KV[:, :].rearrange("p (t n) -> p t n", t=2)
                    nc.scalar.activation(exp_k[:, l, :, :], rows[:, :, 0:P], ACT.Exp, bias=minus1[:, 0:1])
                    nc.scalar.activation(v_r[:, l, :, 0:P], rows[:, :, P:2 * P], ACT.Copy).then_inc(g["v"], 1)
                    act.wait_ge(g["q_cols"], i)
                    nc.scalar.activation(exp_q[:, l, :], QM[:, 0:256], ACT.Exp, bias=minus1[:, 0:1]).then_inc(g["exp_q"], 1)
                if has(2):
                    act.wait_ge(g["att"], i - 1)
                    nc.scalar.activation(den[:, c, :], ND[:, 256:512], ACT.Copy, bias=1e-6).then_inc(g["den"], 1)
                if has(4):
                    act.wait_ge(g["hid_a"], i - 3)
                    nc.scalar.activation(hid[:, c, 0:2, :], WH[:, 0:512].rearrange("p (m t) -> p m t", m=2),
                                         ACT.Relu).then_inc(g["relu_a"], 1)
            act.wait_ge(ones_col, 1)
            pipeline(act, PAIRS, A_DEPTH, 2, body, A_FIRST)

        @on("vector")
        def _(dve):
            g = a_s

            def body(i, s, has, lap):
                c, l = s % 2, (s - 1) % 2
                if has(6):
                    dve.wait_ge(g["w2"], i - 5)
                    bn([W2B[:, 0:P], W2B[:, P:2 * P]], c, 2, g["stats2"])
                if has(0):
                    if isinstance(i, int):
                        for n, (lo, hi) in enumerate(X_PARTS):
                            if lo <= 2 * i < hi or (i == A_FIRST - 1 and lo > 2 * i):
                                dve.wait_ge(x_in[n], 16)
                    bn([tile(xa, i * 2), tile(xa, i * 2 + 1)], c, 0, g["stats0"])
                if has(3):
                    dve.wait_ge(g["wo"], i - 2)
                    bn([WO[:, 0:P], WO[:, P:2 * P]], c, 4, g["stats1"])
                if has(2):
                    dve.wait_ge(g["sums"], i - 1)
                    nc.vector.tensor_tensor(kv[:, c, 0, :], QM[:, 256:256 + P], blk8[:, :], ALU.mult)
                    nc.vector.tensor_scalar(kv[:, c, 1, :], blk8[:, :], QM[:, 256 + P:256 + P + 1], None,
                                            ALU.mult).then_inc(g["masked"], 1)
                if has(5):
                    dve.wait_ge(g["hid_b"], i - 4)
                    nc.vector.tensor_scalar_max(hid[:, l, 2:4, :], WH[:, 512:1024].rearrange("p (m t) -> p m t", m=2),
                                                0.0).then_inc(g["relu_b"], 1)
                if has(0) or has(6):
                    dve.wait_ge(g["rstd"], i + 1)
                if has(6):
                    for t in range(2):
                        last = nc.vector.scalar_tensor_tensor(out=tmp[:, c, t, :], in0=W2B[:, t * P:(t + 1) * P],
                                                              scalar=mean[:, c, 0, 2 + t:3 + t], in1=g2a[:, :],
                                                              op0=ALU.add, op1=ALU.mult)
                    last.then_inc(g["tmp"], 1)
                if has(0):
                    for t in range(2):
                        last = normalise(z0[:, c, t, :], tile(xa, i * 2 + t), c, t)
                    last.then_inc(g["z0"], 1)
                if has(6):
                    dve.wait_ge(g["tmp"], i - 5)
                    dve.wait_ge(g["xres"], i - 5)
                    after(dve, a_stored[c], lap(8) * 16 + 16)
                    for t in range(2):
                        last = nc.vector.scalar_tensor_tensor(out=xout[:, c, t, :], in0=tmp[:, c, t, :],
                                                              scalar=rstd[:, c, 2 + t:3 + t], in1=xres[:, c, t, :],
                                                              op0=ALU.mult, op1=ALU.add)
                    last.then_inc(g["x1"], 1)
                if has(1):
                    dve.wait_ge(g["v"], i)
                    rows = KV[:, :].rearrange("p (t n) -> p t n", t=2)
                    nc.vector.scalar_tensor_tensor(out=k_r[:, l, :, :], in0=exp_k[:, l, :, :], scalar=1.0,
                                                   in1=rows[:, :, 0:P], op0=ALU.min, op1=ALU.max)
                    dve.wait_ge(g["exp_q"], i)
                    nc.vector.scalar_tensor_tensor(out=q_t[:, l, :], in0=exp_q[:, l, :], scalar=1.0,
                                                   in1=QM[:, 0:256], op0=ALU.min, op1=ALU.max).then_inc(g["phi"], 1)
                if has(2):
                    dve.wait_ge(g["den"], i - 1)
                    nc.vector.reciprocal(den[:, c, :], den[:, c, :]).then_inc(g["inv"], 1)
                    dve.wait_ge(g["inv"], i - 1)
                    nc.vector.tensor_tensor(att_t[:, c, :], ND[:, 0:256], den[:, c, :], ALU.mult).then_inc(g["att_t"], 1)
                if has(3):
                    dve.wait_ge(g["rstd1"], i - 2)
                    for t in range(2):
                        last = normalise(z1[:, c, t, :], WO[:, t * P:(t + 1) * P], c, 4 + t)
                    last.then_inc(g["z1"], 1)
            dve.wait_ge(stats_init, 1)
            pipeline(dve, PAIRS, A_DEPTH, 2, body, A_FIRST)

        @on("gpsimd")
        def _(pool):
            g = a_s
            pool.wait_ge(w_a_in, 16 * len(loads_a))

            def body(i, s, has, lap):
                c = s % 2
                if has(0) or has(6):
                    made = [(g["stats2"], i - 5)] * has(6) + [(g["stats0"], i + 1)] * has(0)
                    roots(pool, c, i, 0, 4, made, g["step"], g["rstd"])
                if has(3):
                    roots(pool, c, i - 3, 4, 6, [(g["stats1"], i - 2)], g["step1"], g["rstd1"])
                if has(5):
                    after(pool, g["x1"], i - 6)
                    nc.gpsimd.tensor_tensor(xres[:, (s - 5) % 2, :, :], both(xa, i - 5), b2a[:, :].unsqueeze(1).to_broadcast([P, 2, D]),
                                            ALU.add).then_inc(g["xres"], 1)
            pipeline(pool, PAIRS, A_DEPTH, 2, body, A_FIRST)

        @on("sync")
        def _(sp):
            g = a_s
            rows = x1_dram[:, :].rearrange("(h p s) d -> p h s d", p=P, s=S)

            def body(i, s, has, lap):
                if has(6):
                    sp.wait_ge(g["x1"], i - 5)
                    sp.dma_start(rows[:, :, bass.ds(i - 6, 1), :].rearrange("p h a d -> p h (a d)"),
                                 xout[:, s % 2, :, :]).then_inc(a_stored[s % 2], 16)
            pipeline(sp, PAIRS, A_DEPTH, 2, body, A_FIRST)

        @on("tensor")
        def _(pe):
            pe.wait_ge(w_o_in, 16 * len(loads_o))
            hat_products(pe, hats_f, N_A)

        @on("scalar")
        def _(act):
            hat_copies(act, hats_f, N_A)

        @on("vector")
        def _(dve):
            dve.wait_ge(w_o_in, 16 * len(loads_o))
            hat_copies(dve, hats_f, N_A, of_vector=True)

        G_PARTS = ((0, 2), (2, 12), (12, 22), (22, 32))
        m_s = {k: sem("m_" + k) for k in (
            "stats0", "stats1", "step", "rstd", "shift", "z0", "z1", "turned", "zt", "qk", "kx", "v_rows", "v", "s",
            "masked", "max", "centred", "exp", "sum", "prob", "p_t", "att", "att_t", "wo", "wo_kept", "gate", "gate_read",
            "best", "seen", "gone0", "hot", "rank", "placed", "pos", "pay_z", "pay_x", "pay_t")}
        sorted_ = [sem(f"m_sorted{k}") for k in range(3)]
        x_back = [sem(f"m_x{k}") for k in range(len(G_PARTS))]
        wb_in = sem("wb_in")
        totals, cleared = sem("m_totals"), sem("m_cleared")
        LAST = (PAIRS - 1) % 3
        M_BODIES = PAIRS + 4

        def clear_p(dve, hats):
            dve.wait_ge(hat_kept, hats)
            nc.vector.memset(p_t[:, :, :, :, :], 0.0).then_inc(p_cleared, 1)

        def clear_k(pool, hats):
            pool.wait_ge(hat_kept, hats)
            nc.gpsimd.memset(k_x[:, :, :, :, :, :], 0.0).then_inc(k_cleared, 1)

        def attention_block(n, src_dram, stored_before):
            o, ob = n * PAIRS, n * M_BODIES
            DEPTH, FIRST = 8, 7
            TT, QK, VB, SB, WO, AV, GB, RB = (bank[k] for k in range(8))

            def laps(k):
                return 32 * n * len(range(k, PAIRS, 3))

            @on("sync")
            def _(sp):
                for sem_, count in stored_before:
                    sp.wait_ge(sem_, count)
                rows = src_dram[:, :].rearrange("(t p) d -> p t d", p=P)
                for k, (lo, hi) in enumerate(G_PARTS):
                    sp.dma_start(xa[:, lo:hi, :], rows[:, lo:hi, :]).then_inc(x_back[k], 16)

            @on("tensor")
            def _(pe):
                g = m_s

                def body(i, s, has, lap):
                    c1, c2, c3, c4 = ((s - k) % 3 for k in (1, 2, 3, 4))
                    if has(2):
                        pe.wait_ge(g["kx"], o + i - 1)
                        after(pe, g["masked"], o + i - 2)
                        for t in range(2):
                            for q in range(4):
                                last = nc.tensor.matmul(SB[32 * q:32 * q + 32, t * P:(t + 1) * P],
                                                        q_t[:, c2, t * P + 32 * q:t * P + 32 * q + 32],
                                                        k_x[:, c2, t, q, :, :].rearrange("p h k -> p (h k)"),
                                                        start=True, stop=True)
                        last.then_inc(g["s"], 1)
                    if has(4):
                        pe.wait_ge(g["att_t"], o + i - 3)
                        after(pe, g["wo_kept"], o + i - 4)
                        for t in range(2):
                            cut = slice(t * P, (t + 1) * P)
                            nc.tensor.matmul(WO[:, cut], att_t[:, c4, cut], wf_o[:, :], start=True, stop=False)
                            last = nc.tensor.matmul(WO[:, cut], zt[:, c4, 0, cut], rf0[:, :], start=False, stop=True)
                        last.then_inc(g["wo"], 1)
                    if has(1) or has(5):
                        after(pe, g["zt"], ob + i - 1)
                        if has(1):
                            pe.wait_ge(g["z0"], o + i)
                            for t in range(2):
                                last = nc.tensor.transpose(TT[:, t * P:(t + 1) * P], z0[:, c1, t, :], ident[:, :])
                        if has(5):
                            pe.wait_ge(g["z1"], o + i - 4)
                            for t in range(2):
                                last = nc.tensor.transpose(TT[:, 256 + t * P:256 + (t + 1) * P], z1[:, c2, t, :],
                                                           ident[:, :])
                        last.then_inc(g["turned"], 1)
                    if has(7):
                        pe.wait_ge(g["hot"], o + i - 6)
                        after(pe, g["placed"], o + i - 7)
                        nc.tensor.matmul(RB[:, 0:2 * E], lower[:, :], hot[:, c1, :, :].rearrange("p t e -> p (t e)"),
                                         start=True, stop=False)
                        nc.tensor.matmul(RB[:, 0:2 * E], ones[:, :], gone[:, c1, :, :].rearrange("p t e -> p (t e)"),
                                         start=False, stop=True).then_inc(g["rank"], 1)
                    if has(1):
                        pe.wait_ge(g["zt"], ob + i)
                        after(pe, g["kx"], o + i - 1)
                        nc.tensor.matmul(QK[:, 0:256], wf_qkv[:, 0:D], zt[:, c1, 0, :], start=True, stop=True)
                        nc.tensor.matmul(QK[:, 256:512], wf_qkv[:, D:2 * D], zt[:, c1, 0, :], start=True,
                                         stop=True).then_inc(g["qk"], 1)
                        after(pe, g["v"], o + i - 1)
                        for t in range(2):
                            last = nc.tensor.matmul(VB[:, t * P:(t + 1) * P], zt[:, c1, 0, t * P:(t + 1) * P],
                                                    wf_qkv[:, 2 * D:], start=True, stop=True)
                        last.then_inc(g["v_rows"], 1)
                    if has(5):
                        if not has(1):
                            pe.wait_ge(g["zt"], ob + i)
                        after(pe, g["gate_read"], o + i - 5)
                        for t in range(2):
                            last = nc.tensor.matmul(GB[:, t * E:(t + 1) * E], zt[:, c1, 1, t * P:(t + 1) * P], wg[:, :],
                                                    start=True, stop=True)
                        last.then_inc(g["gate"], 1)
                    if has(3):
                        pe.wait_ge(g["p_t"], o + i - 2)
                        pe.wait_ge(g["v"], o + i - 2)
                        after(pe, g["att_t"], o + i - 3)
                        for t in range(2):
                            for h in range(HM):
                                last = nc.tensor.matmul(AV[DM * h:DM * (h + 1), t * P:(t + 1) * P],
                                                        v_r[:, c3, t, DM * h:DM * (h + 1)], p_t[:, c3, t, h, :],
                                                        start=True, stop=True)
                        last.then_inc(g["att"], 1)
                pipeline(pe, PAIRS, DEPTH, 3, body, FIRST)
                pe.wait_ge(g["placed"], o + PAIRS)
                nc.tensor.matmul(RB[:, 0:E], ones[:, :], gone[:, LAST, 1, :], start=True, stop=False)
                nc.tensor.matmul(RB[:, 0:E], ones[:, :], hot[:, LAST, 1, :], start=False, stop=True).then_inc(totals, 1)

            @on("scalar")
            def _(act):
                g = m_s

                def body(i, s, has, lap):
                    c1, c2, c3 = ((s - k) % 3 for k in (1, 2, 3))
                    if has(4):
                        act.wait_ge(g["wo"], o + i - 3)
                        nc.scalar.activation(tmp[:, c1, :, :].rearrange("p t d -> p (t d)"), WO[:, 0:256],
                                             ACT.Copy).then_inc(g["wo_kept"], 1)
                    if has(1) or has(5):
                        act.wait_ge(g["turned"], ob + i)
                        lo, hi = (0 if has(1) else 1), (2 if has(5) else 1)
                        nc.scalar.activation(zt[:, c1, lo:hi, :],
                                             TT[:, 256 * lo:256 * hi].rearrange("p (n t) -> p n t", n=hi - lo),
                                             ACT.Copy, bias=HAT).then_inc(g["zt"], 1)
                    if has(6):
                        after(act, sorted_[s % 3], lap(6) * 32 + laps(s % 3))
                        nc.scalar.activation(pay[:, s % 3, :, 0:D], z1[:, s % 3, :, :], ACT.Copy).then_inc(g["pay_z"], 1)
                    if has(1):
                        act.wait_ge(g["qk"], o + i)
                        nc.scalar.activation(q_t[:, c1, :], QK[:, 0:256], ACT.Copy, scale=DM ** -0.5)
                        if isinstance(i, int) and i == 1:
                            act.wait_ge(k_cleared, n + 1)
                        for h in range(HM):
                            rows = slice(DM * h, DM * (h + 1))
                            last = nc.scalar.activation(k_x[rows, c1, :, :, h, :].rearrange("p t q k -> p (t q) k"),
                                                        QK[rows, 256:512].rearrange("p (n k) -> p n k", k=32), ACT.Copy)
                        last.then_inc(g["kx"], 1)
                        act.wait_ge(g["v_rows"], o + i)
                        nc.scalar.activation(v_r[:, c1, :, 0:P], VB[:, 0:256].rearrange("p (t n) -> p t n", t=2),
                                             ACT.Copy).then_inc(g["v"], 1)
                    if has(3):
                        act.wait_ge(g["att"], o + i - 2)
                        nc.scalar.activation(att_t[:, c3, :], AV[:, 0:256], ACT.Copy).then_inc(g["att_t"], 1)
                    if has(2):
                        act.wait_ge(g["centred"], o + i - 1)
                        nc.scalar.activation(sc[:, c2, :, :, :], sc[:, c2, :, :, :], ACT.Exp).then_inc(g["exp"], 1)
                    if has(0):
                        act.wait_ge(g["shift"], o + i + 1)
                        for t in range(2):
                            last = nc.scalar.activation(z0[:, s % 3, t, :], tile(xa, i * 2 + t), ACT.Identity,
                                                        bias=shift[:, s % 3, t:t + 1], scale=rstd[:, s % 3, t:t + 1])
                        last.then_inc(g["z0"], 1)
                pipeline(act, PAIRS, DEPTH - 1, 3, body, FIRST)

            @on("vector")
            def _(dve):
                g = m_s

                def body(i, s, has, lap):
                    c, c1, c2, c3, c4 = ((s - k) % 3 for k in (0, 1, 2, 3, 4))
                    if has(0):
                        if isinstance(i, int):
                            for k, (lo, _) in enumerate(G_PARTS):
                                if 2 * i == lo or (i == FIRST - 1 and lo > 2 * i):
                                    dve.wait_ge(x_back[k], 16 * (2 * n + 1))
                        bn([tile(xa, i * 2), tile(xa, i * 2 + 1)], c, 0, g["stats0"])
                    if has(4):
                        dve.wait_ge(g["wo_kept"], o + i - 3)
                        bn([tmp[:, c4, 0, :], tmp[:, c4, 1, :]], c, 2, g["stats1"])
                    logits = GB[:, 0:2 * E].rearrange("p (t e) -> p t e", t=2)
                    weight = rank_w[:, :].unsqueeze(1).to_broadcast([P, 2, E])
                    p = sc[:, c3, :, :, :].rearrange("p t h k -> p (t h) k")
                    raw = sc[:, c2, :, :, :].rearrange("p t h k -> p (t h) k")
                    if has(3):
                        dve.wait_ge(g["exp"], o + i - 2)
                        nc.vector.tensor_reduce(out=sums[:, c3, :], in_=p, axis=AX.X, op=ALU.add).then_inc(g["sum"], 1)
                    if has(6):
                        dve.wait_ge(g["gate"], o + i - 5)
                        nc.vector.tensor_reduce(out=best[:, :], in_=logits, axis=AX.X, op=ALU.max).then_inc(g["best"], 1)
                    if has(7):
                        dve.wait_ge(g["rank"], o + i - 6)
                        nc.vector.tensor_tensor(place[:, :, :], RB[:, 0:2 * E].rearrange("p (t e) -> p t e", t=2),
                                                hot[:, c1, :, :], ALU.mult).then_inc(g["placed"], 1)
                    if has(3):
                        dve.wait_ge(g["sum"], 2 * o + i * 2 - 5)
                        nc.vector.reciprocal(inv[:, c3, :], sums[:, c3, :]).then_inc(g["sum"], 1)
                    if has(6):
                        dve.wait_ge(g["best"], 2 * o + i * 2 - 11)
                        nc.vector.tensor_tensor(seen[:, :, :], logits, best[:, :].unsqueeze(2).to_broadcast([P, 2, E]),
                                                ALU.is_ge).then_inc(g["gate_read"], 1)
                    if has(3):
                        dve.wait_ge(g["sum"], 2 * o + i * 2 - 4)
                        nc.vector.tensor_tensor(p, p, inv[:, c3, :].unsqueeze(2).to_broadcast([P, 2 * HM, 32]),
                                                ALU.mult).then_inc(g["prob"], 1)
                    if has(6):
                        dve.wait_ge(g["gate_read"], o + i - 5)
                        nc.vector.tensor_tensor(seen[:, :, :], seen[:, :, :], weight, ALU.mult).then_inc(g["seen"], 1)
                    if has(3):
                        dve.wait_ge(g["prob"], o + i - 2)
                        for q in range(4):
                            rows = slice(32 * q, 32 * q + 32)
                            last = nc.vector.transpose(
                                p_t[rows, c3, :, :, 32 * q:32 * q + 32].rearrange("p t h k -> p (t h) k"),
                                sc[rows, c3, :, :, :].rearrange("p t h k -> p (t h) k"))
                        last.then_inc(g["p_t"], 1)
                    if has(2):
                        dve.wait_ge(g["s"], o + i - 1)
                        nc.vector.tensor_tensor(raw, SB[:, 0:256].rearrange("p (n k) -> p n k", k=32),
                                                far[:, :].unsqueeze(1).to_broadcast([P, 2 * HM, 32]),
                                                ALU.add).then_inc(g["masked"], 1)
                    if has(6):
                        dve.wait_ge(g["seen"], o + i - 5)
                        nc.vector.tensor_reduce(out=best[:, :], in_=seen[:, :, :], axis=AX.X, op=ALU.max).then_inc(g["best"], 1)
                    if has(7):
                        dve.wait_ge(g["placed"], o + i - 6)
                        after(dve, sorted_[c1], lap(7) * 32 + laps(c1))
                        nc.vector.tensor_reduce(out=pos[:, c1, :], in_=place[:, :, :], axis=AX.X,
                                                op=ALU.max).then_inc(g["pos"], 1)
                    if has(2):
                        dve.wait_ge(g["masked"], o + i - 1)
                        nc.vector.tensor_reduce(out=mx[:, c2, :], in_=raw, axis=AX.X, op=ALU.max).then_inc(g["max"], 1)
                    if has(6):
                        dve.wait_ge(g["best"], 2 * o + i * 2 - 10)
                        nc.vector.tensor_tensor(hot[:, c, :, :], weight, best[:, :].unsqueeze(2).to_broadcast([P, 2, E]),
                                                ALU.is_equal)
                        nc.vector.tensor_tensor(gone[:, c, 0, :], gone[:, c1, 1, :], hot[:, c1, 1, :],
                                                ALU.add).then_inc(g["gone0"], 1)
                    if has(2):
                        dve.wait_ge(g["max"], o + i - 1)
                        nc.vector.tensor_tensor(raw, raw, mx[:, c2, :].unsqueeze(2).to_broadcast([P, 2 * HM, 32]),
                                                ALU.subtract).then_inc(g["centred"], 1)
                    if has(6):
                        after(dve, sorted_[c], lap(6) * 32 + laps(c))
                        nc.vector.tensor_copy(pay[:, c, :, 2 * D:].rearrange("p t a -> p (t a)").bitcast(U32),
                                              token[:, bass.ds(i * 2 - 12, 2)]).then_inc(g["pay_t"], 1)
                        dve.wait_ge(g["gone0"], o + i - 5)
                        nc.vector.tensor_tensor(gone[:, c, 1, :], gone[:, c, 0, :], hot[:, c, 0, :],
                                                ALU.add).then_inc(g["hot"], 1)
                    if has(4):
                        dve.wait_ge(g["rstd"], ob + i + 1)
                    if has(4):
                        after(dve, g["pay_z"], o + i - 6)
                        for t in range(2):
                            last = nc.vector.tensor_scalar(z1[:, c4, t, :], tmp[:, c4, t, :],
                                                           mean[:, c, 0, 2 + t:3 + t], rstd[:, c, 2 + t:3 + t],
                                                           ALU.add, ALU.mult)
                        last.then_inc(g["z1"], 1)
                    if isinstance(i, int) and i == 0:
                        if n == 0:
                            clear_p(dve, N_F)
                        dve.wait_ge(p_cleared, n + 1)
                if n > 0:
                    dve.wait_ge(totals, n)
                else:
                    dve.wait_ge(tokens_made, 1)
                nc.vector.memset(hot[:, 2, 1, :], 0.0).then_inc(cleared, 1)
                nc.vector.tensor_copy(gone[:, 2, 1, :], rooms_row[:, :]).then_inc(cleared, 1)
                dve.wait_ge(cleared, 2 * n + 2)
                pipeline(dve, PAIRS, DEPTH, 3, body, FIRST)

            @on("gpsimd")
            def _(pool):
                g = m_s

                def body(i, s, has, lap):
                    made = [(g["stats0"], o + i + 1)] * has(0) + [(g["stats1"], o + i - 3)] * has(4)
                    if has(0) or has(4):
                        roots(pool, s % 3, ob + i, 0, 4, made, g["step"], g["rstd"])
                    if has(0):
                        pool.wait_ge(g["rstd"], ob + i + 1)
                        nc.gpsimd.tensor_tensor(shift[:, s % 3, :], mean[:, s % 3, 0, 0:2], rstd[:, s % 3, 0:2],
                                                ALU.mult).then_inc(g["shift"], 1)
                    if n == 0 and isinstance(i, int) and i == 0:
                        clear_k(pool, N_F)
                    if has(7):
                        for made in ("pay_z", "pay_x", "pay_t", "pos"):
                            pool.wait_ge(g[made], o + i - 6)
                    if has(6):
                        after(pool, sorted_[s % 3], lap(6) * 32 + laps(s % 3))
                        nc.gpsimd.tensor_tensor(pay[:, s % 3, :, D:2 * D], both(xa, i - 6),
                                                b2f[:, :].unsqueeze(1).to_broadcast([P, 2, D]), ALU.add).then_inc(g["pay_x"], 1)
                    if has(7):
                        c = (s - 7) % 3
                        for t in range(2):
                            nc.gpsimd.indirect_dma_start(
                                sorted_dram[n][:, :], bass.IndirectOffsetOnAxis(ap=pos[:, c, t:t + 1], axis=0),
                                pay[:, c, t, :], None).then_inc(sorted_[c], 16)
                pipeline(pool, PAIRS, DEPTH, 3, body, FIRST)

        r_step, padded_at, tabled, padded = (sem("r_" + k) for k in ("step", "padded_at", "tabled", "padded"))
        R_STEPS = 14
        REPEAT = 16
        assert ET - NT < REPEAT <= NT

        def table(n):
            @on("vector")
            def _(dve):
                made = [n * R_STEPS]

                def link(instruction):
                    made[0] += 1
                    instruction.then_inc(r_step, 1)
                    dve.wait_ge(r_step, made[0])

                def over_j(x):
                    return x.unsqueeze(1).to_broadcast([P, ET, E])

                dve.wait_ge(totals, n + 1)
                link(nc.vector.tensor_copy(room_end[:, :], bank[7][:, 0:E]))
                nc.vector.tensor_copy(pad_at[:, :], room_end[:, :]).then_inc(padded_at, 1)
                link(nc.vector.tensor_tensor(room_end[:, :], room_end[:, :], rooms[:, :], ALU.subtract))
                link(nc.vector.tensor_tensor(over[:, :, :], room_end[:, :].unsqueeze(2).to_broadcast([P, E, NT]),
                                             steps[:, :].unsqueeze(1).to_broadcast([P, E, NT]), ALU.is_gt))
                link(nc.vector.tensor_reduce(out=n_tiles[:, :], in_=over[:, :, :], axis=AX.X, op=ALU.add))
                link(nc.vector.tensor_tensor(ends_m[:, :, :], upto[:, :, :], n_tiles[:, :].unsqueeze(1).to_broadcast([P, E, E]),
                                             ALU.mult))
                link(nc.vector.tensor_reduce(out=ends[:, :], in_=ends_m[:, :, :], axis=AX.X, op=ALU.add))
                link(nc.vector.tensor_scalar(beyond[:, :], tile_no[:, :], ends[:, E - 1:E], float(-REPEAT), ALU.is_ge,
                                             ALU.mult))
                link(nc.vector.tensor_tensor(tile_of[:, :], tile_no[:, :], beyond[:, :], ALU.add))
                link(nc.vector.tensor_tensor(owner_m[:, :, :], tile_of[:, :].unsqueeze(2).to_broadcast([P, ET, E]),
                                             over_j(ends[:, :]), ALU.is_ge))
                link(nc.vector.tensor_reduce(out=owner_f[:, :], in_=owner_m[:, :, :], axis=AX.X, op=ALU.add))
                nc.vector.tensor_copy(owner[:, :], owner_f[:, :]).then_inc(tabled, 1)
                link(nc.vector.tensor_scalar(skip[:, :], n_tiles[:, :], float(-P), float(ROOM), ALU.mult, ALU.add))
                link(nc.vector.tensor_tensor(skip_m[:, :, :], owner_m[:, :, :], over_j(skip[:, :]), ALU.mult))
                link(nc.vector.tensor_reduce(out=first_f[:, :], in_=skip_m[:, :, :], axis=AX.X, op=ALU.add))
                link(nc.vector.scalar_tensor_tensor(out=first_f[:, :], in0=tile_of[:, :], scalar=float(P),
                                                    in1=first_f[:, :], op0=ALU.mult, op1=ALU.add))
                nc.vector.tensor_scalar_add(first_row[:, :], first_f[:, :], float(P)).then_inc(tabled, 1)
                assert made[0] == (n + 1) * R_STEPS, made

            @on("sync")
            def _(sp):
                pads(sp, 0)

            @on("scalar")
            def _(act):
                pads(act, 1)

            def pads(eng, parity):
                if n == 0:
                    eng.wait_ge(firsts_out, 16 * 2 * 2)
                for k in range(3):
                    eng.wait_ge(sorted_[k], 32 * (n + 1) * len(range(k, PAIRS, 3)))
                eng.wait_ge(padded_at, n + 1)
                for e in range(parity, E, 2):
                    end = eng.value_load(pad_at[0:1, e:e + 1], min_val=P + e * ROOM, max_val=P + e * ROOM + T)
                    eng.dma_start(sorted_dram[n][bass.ds(end, P), :],
                                  sorted_dram[n][bass.ds((end - 1) // P * P, 1), :].to_broadcast([P, PAY])).then_inc(padded, 16)

        e_s = {k: sem("e_" + k) for k in (
            "turned", "zt", "w1", "w2", "hid_a", "hid_b", "relu_a", "relu_b", "v", "stats", "agg", "var",
            "rstd", "tmp", "dest", "y")}
        loaded = [sem(f"e_loaded{k}") for k in range(ZS)]
        stored = [sem(f"e_stored{k}") for k in range(3)]

        def times(k, slots, n):
            return 16 * n * len(range(k, ET, slots))

        def experts(n, target):
            o = n * ET
            DEPTH, FIRST = 6, 12
            TB, HA_, HB_ = bank[0], bank[1], bank[2]
            VB = [bank[3], bank[4], bank[5]]

            @on("gpsimd")
            def _(pool):
                g = e_s

                def body(i, s, has, lap):
                    if has(5):
                        pool.wait_ge(g["y"], o + i - 4)
                        pool.wait_ge(g["dest"], o + i - 4)
                    if has(3):
                        pool.wait_ge(g["var"], o + i - 2)
                        nc.gpsimd.tensor_tensor(rstd[:, s % 3, 0:1], var_e[:, s % 3, :], half_neg[:, 0:1],
                                                ALU.pow).then_inc(g["rstd"], 1)
                    if has(5):
                        c = (s - 5) % 3
                        nc.gpsimd.indirect_dma_start(
                            target, bass.IndirectOffsetOnAxis(ap=dest[:, c, :], axis=0), xout[:, c, 0, :],
                            None).then_inc(stored[(s - 5) % 3], 16)
                pipeline(pool, ET, DEPTH, 3, body, 6)

            @on("sync")
            def _(sp):
                g = e_s
                sp.wait_ge(padded, (n + 1) * 16 * E)
                sp.wait_ge(tabled, (n + 1) * 2)

                def body(i, s, has, lap):
                    after(sp, g["y"], o + i + 1 - ZS)
                    after(sp, g["dest"], o + i + 1 - ZS)
                    at = sp.value_load(first_row[0:1, bass.ds(i, 1)], min_val=0, max_val=E * ROOM)
                    sp.dma_start(zs[:, s % ZS, :], sorted_dram[n][bass.ds(at, P), :]).then_inc(loaded[s % ZS], 16)
                pipeline(sp, ET, 1, ZS, body, FIRST)

            @on("tensor")
            def _(pe):
                g = e_s

                def body(i, s, has, lap):
                    c, c1, c2 = s % 3, (s - 1) % 3, (s - 2) % 3
                    if has(0):
                        pe.wait_ge(loaded[s % ZS], lap(0) * 16 + (times(s % ZS, ZS, n) + 16))
                        after(pe, g["zt"], o + i)
                        nc.tensor.transpose(TB[:, 0:P], zs[:, s % ZS, 0:D], ident[:, :]).then_inc(g["turned"], 1)
                    if has(1):
                        pe.wait_ge(g["zt"], o + i)
                        pe.wait_ge(g["w1"], o + i)
                        for m in range(FC):
                            if m == 0:
                                after(pe, g["relu_a"], o + i - 1)
                            if m == 2:
                                after(pe, g["relu_b"], o + i - 1)
                            to = HA_ if m < 2 else HB_
                            last = nc.tensor.matmul(to[:, (m % 2) * P:(m % 2 + 1) * P], we_t[:, c1, m * P:(m + 1) * P],
                                                    zt[:, c1, 0, 0:P], start=True, stop=True)
                            if m == 1:
                                last.then_inc(g["hid_a"], 1)
                        last.then_inc(g["hid_b"], 1)
                    if has(2):
                        pe.wait_ge(g["relu_a"], o + i - 1)
                        pe.wait_ge(g["relu_b"], o + i - 1)
                        pe.wait_ge(g["w2"], o + i - 1)
                        after(pe, g["tmp"], o + i - 4)
                        for m in range(FC):
                            nc.tensor.matmul(VB[c2][:, 0:P], hid_e[:, c2, m, :], we_t[:, c2, F + m * P:F + (m + 1) * P],
                                             start=(m == 0), stop=False)
                        nc.tensor.matmul(VB[c2][:, 0:P], zt[:, c2, 0, 0:P], we_t[:, c2, 2 * F:], start=False,
                                         stop=True).then_inc(g["v"], 1)
                pipeline(pe, ET, 3, ZS, body, FIRST)

            @on("scalar")
            def _(act):
                g = e_s

                def body(i, s, has, lap):
                    c, c1 = s % 3, (s - 1) % 3
                    if has(0):
                        act.wait_ge(g["turned"], o + i + 1)
                        nc.scalar.activation(zt[:, c, 0, 0:P], TB[:, 0:P], ACT.Copy, bias=HAT).then_inc(g["zt"], 1)
                    if has(1):
                        act.wait_ge(g["hid_a"], o + i)
                        nc.scalar.activation(hid_e[:, c1, 0:2, :], HA_[:, 0:256].rearrange("p (m t) -> p m t", m=2),
                                             ACT.Relu).then_inc(g["relu_a"], 1)
                    if has(0):
                        after(act, g["hid_b"], o + i - 2)
                        e = act.value_load(owner[0:1, bass.ds(i, 1)], min_val=0, max_val=E - 1)
                        nc.scalar.activation(we_t[:, c, 0:F], we[:, bass.ds(e, 1), 0:F].rearrange("p a n -> p (a n)"),
                                             ACT.Copy).then_inc(g["w1"], 1)
                act.wait_ge(tabled, n * 2 + 1)
                pipeline(act, ET, 2, 3, body, 6)

            @on("vector")
            def _(dve):
                g = e_s

                def body(i, s, has, lap):
                    c, c1 = s % 3, (s - 1) % 3
                    if has(0):
                        e = dve.value_load(owner[0:1, bass.ds(i, 1)], min_val=0, max_val=E - 1)
                    if has(3):
                        dve.wait_ge(g["v"], o + i - 2)
                        nc.vector.bn_stats(stats[:, c, 0, :], VB[c][:, 0:P]).then_inc(g["stats"], 1)
                        dve.wait_ge(g["stats"], o + i - 2)
                    if has(1):
                        dve.wait_ge(g["hid_b"], o + i)
                        nc.vector.tensor_scalar_max(hid_e[:, c1, 2:4, :], HB_[:, 0:256].rearrange("p (m t) -> p m t", m=2),
                                                    0.0).then_inc(g["relu_b"], 1)
                    if has(3):
                        nc.vector.bn_aggr(mv[:, c, :], stats[:, c, 0, :]).then_inc(g["agg"], 1)
                    if has(4):
                        dve.wait_ge(g["rstd"], o + i - 3)
                        nc.vector.scalar_tensor_tensor(out=tmp[:, c1, 0, :], in0=VB[c1][:, 0:P], scalar=mv[:, c1, 0:1],
                                                       in1=g2f[:, :], op0=ALU.subtract, op1=ALU.mult).then_inc(g["tmp"], 1)
                    if has(3):
                        dve.wait_ge(g["agg"], o + i - 2)
                        nc.vector.tensor_scalar_add(var_e[:, c, :], mv[:, c, 1:2], EPS).then_inc(g["var"], 1)
                    if has(4):
                        dve.wait_ge(g["tmp"], o + i - 3)
                        if has(7):
                            dve.wait_ge(stored[(s - 7) % 3], lap(7, 3) * 16 + (times((s - 7) % 3, 3, n) + 16))
                        row = zs[:, (s - 4) % ZS, :]
                        nc.vector.tensor_copy(dest[:, c1, :], row[:, 2 * D:].bitcast(U32)).then_inc(g["dest"], 1)
                        nc.vector.scalar_tensor_tensor(out=xout[:, c1, 0, :], in0=tmp[:, c1, 0, :],
                                                       scalar=rstd[:, c1, 0:1], in1=row[:, D:2 * D], op0=ALU.mult,
                                                       op1=ALU.add).then_inc(g["y"], 1)
                    if has(0):
                        after(dve, g["v"], o + i - 2)
                        nc.vector.tensor_copy(we_t[:, c, F:], we[:, bass.ds(e, 1), F:].rearrange("p a n -> p (a n)"))\
                            .then_inc(g["w2"], 1)
                dve.wait_ge(tabled, n * 2 + 1)
                pipeline(dve, ET, 5, ZS, body, FIRST)

        def block_b():
            b_s = {k: sem("b_" + k) for k in (
                "stats0", "step", "rstd", "z0", "z", "turned", "zt", "gram", "gram_kept", "u", "u_a", "u_b", "bo", "m", "m_kept",
                "out", "x3")}
            b_stored = [sem(f"b_stored{k}") for k in range(3)]
            DEPTH, FIRST = 5, 7
            TB, MB, OB = bank[0], bank[1], bank[2]
            G_COLS = slice(256, 384)

            @on("sync")
            def _(sp):
                for k in range(3):
                    sp.wait_ge(stored[k], times(k, 3, 1))
                rows = x2_dram[:, :].rearrange("(t p) d -> p t d", p=P)
                for k, (lo, hi) in enumerate(G_PARTS):
                    sp.dma_start(xa[:, lo:hi, :], rows[:, lo:hi, :]).then_inc(x_back[k], 16)
                x3_rows = x3_dram[:, :].rearrange("(h p s) d -> p h s d", p=P, s=S)

                def body(i, s, has, lap):
                    if has(4):
                        sp.wait_ge(b_s["x3"], i - 3)
                        sp.dma_start(x3_rows[:, :, bass.ds(i - 4, 1), :].rearrange("p h a d -> p h (a d)"),
                                     xout[:, (s - 4) % 3, :, :]).then_inc(b_stored[(s - 4) % 3], 16)
                pipeline(sp, PAIRS, DEPTH, 3, body, FIRST)

            @on("gpsimd")
            def _(pool):
                g = b_s

                def body(i, s, has, lap):
                    roots(pool, s % 3, i, 0, 2, [(g["stats0"], i + 1)], g["step"], g["rstd"])
                    pool.wait_ge(g["z0"], i + 1)
                    nc.gpsimd.tensor_tensor(z1[:, s % 3, :, :], z0[:, s % 3, :, :], hats[:, :, :], ALU.add).then_inc(g["z"], 1)
                pipeline(pool, PAIRS, 1, 3, body, FIRST)
                clear_k(pool, N_HATS)

            @on("tensor")
            def _(pe):
                g = b_s

                def heads(some, c):
                    for h in some:
                        last = nc.tensor.matmul(MB[:, 0:P], qk_t[:, h, :], u_sb[:, c, h * D:(h + 1) * D],
                                                start=(h == 0), stop=(h == HB - 1))
                    return last

                def body(i, s, has, lap):
                    c1, c2, c3 = ((s - k) % 3 for k in (1, 2, 3))
                    if has(2):
                        pe.wait_ge(g["gram_kept"], i - 1)
                        after(pe, g["u_a"], i - 2)
                        after(pe, g["u_b"], i - 2)
                        for k in range(4):
                            last = nc.tensor.matmul(wide[:, 512 * k:512 * (k + 1)], gram[:, c2, :],
                                                    vo[:, 4 * k:4 * k + 4, :].rearrange("p h d -> p (h d)"),
                                                    start=True, stop=True)
                            if k == 1:
                                last.then_inc(g["u"], 1)
                        last.then_inc(g["u"], 1)
                    if has(4):
                        pe.wait_ge(g["m_kept"], i - 3)
                        after(pe, g["x3"], i - 4)
                        for t in range(2):
                            last = nc.tensor.matmul(OB[:, t * P:(t + 1) * P], zt[:, c1, 0, t * P:(t + 1) * P],
                                                    m_sb[:, c1, :], start=True, stop=True)
                        last.then_inc(g["out"], 1)
                    if has(1):
                        pe.wait_ge(g["z"], i)
                        after(pe, g["gram_kept"], i - 1)
                        for t in range(2):
                            last = nc.tensor.transpose(TB[:, t * P:(t + 1) * P], z1[:, c1, t, :], ident[:, :])
                        last.then_inc(g["turned"], 1)
                    if has(3):
                        pe.wait_ge(g["u_a"], i - 2)
                        pe.wait_ge(g["u_b"], i - 2)
                        after(pe, g["m_kept"], i - 3)
                        heads(range(HB // 2), c3)
                    if has(1):
                        pe.wait_ge(g["zt"], i)
                        for t in range(2):
                            last = nc.tensor.matmul(TB[:, G_COLS], z1[:, c1, t, :], z1[:, c1, t, :], start=(t == 0),
                                                    stop=(t == 1))
                        last.then_inc(g["gram"], 1)
                    if has(3):
                        heads(range(HB // 2, HB), c3).then_inc(g["m"], 1)
                pipeline(pe, PAIRS, DEPTH, 3, body, FIRST)

            @on("scalar")
            def _(act):
                g = b_s

                def body(i, s, has, lap):
                    c1, c2, c3 = ((s - k) % 3 for k in (1, 2, 3))
                    if has(2):
                        act.wait_ge(g["u"], i * 2 - 3)
                        nc.scalar.activation(u_sb[:, c2, 0:1024], wide[:, 0:1024], ACT.Copy).then_inc(g["u_a"], 1)
                    if has(1):
                        act.wait_ge(g["turned"], i)
                        nc.scalar.activation(zt[:, c1, 0, :], TB[:, 0:256], ACT.Copy).then_inc(g["zt"], 1)
                        act.wait_ge(g["gram"], i)
                        nc.scalar.activation(gram[:, c1, :], TB[:, G_COLS], ACT.Copy).then_inc(g["gram_kept"], 1)
                pipeline(act, PAIRS, DEPTH - 2, 3, body, FIRST)

            @on("vector")
            def _(dve):
                g = b_s

                def body(i, s, has, lap):
                    c, c1, c2 = ((s - k) % 3 for k in (0, 1, 2))
                    if has(4):
                        dve.wait_ge(g["m"], i - 3)
                        nc.vector.tensor_tensor(m_sb[:, c1, :], MB[:, 0:P], bo[:, :], ALU.add).then_inc(g["m_kept"], 1)
                    if has(0):
                        if isinstance(i, int):
                            for k, (lo, _) in enumerate(G_PARTS):
                                if 2 * i == lo or (i == FIRST - 1 and lo > 2 * i):
                                    dve.wait_ge(x_back[k], 32)
                        bn([tile(xa, i * 2), tile(xa, i * 2 + 1)], c, 0, g["stats0"])
                    if has(2):
                        dve.wait_ge(g["u"], i * 2 - 2)
                        nc.vector.tensor_copy(u_sb[:, c2, 1024:2048], wide[:, 1024:2048]).then_inc(g["u_b"], 1)
                    if has(4):
                        dve.wait_ge(g["out"], i - 3)
                        after(dve, b_stored[c1], lap(4) * 16)
                        nc.vector.tensor_tensor(xout[:, c1, :, :], OB[:, 0:256].rearrange("p (t d) -> p t d", t=2),
                                                both(xa, i - 4), ALU.add).then_inc(g["x3"], 1)
                    if has(0):
                        dve.wait_ge(g["rstd"], i + 1)
                        for t in range(2):
                            last = normalise(z0[:, c, t, :], tile(xa, i * 2 + t), c, t)
                        last.then_inc(g["z0"], 1)
                dve.wait_ge(w_o_in, 16 * len(loads_o))
                nc.vector.tensor_scalar_mul(bo[:, :], bo[:, :], ROW).then_inc(g["bo"], 1)
                dve.wait_ge(g["bo"], 1)
                pipeline(dve, PAIRS, DEPTH, 3, body, FIRST)
                clear_p(dve, N_HATS)
            return [(b_stored[k], 16 * len(range(k, PAIRS, 3))) for k in range(3)]

        a_done = [(s_, 16 * (PAIRS // 2)) for s_ in a_stored]
        attention_block(0, x1_dram, a_done)

        @on("sync")
        def _(sp):
            sp.wait_ge(m_s["att"], PAIRS)
            for m, w in enumerate(("Wq", "Wk", "Wv")):
                sp.dma_start(wb_raw[:, m, :], b[w]).then_inc(wb_in, 16)

        @on("tensor")
        def _(pe):
            pe.wait_ge(wb_in, 16 * 3)
            pe.wait_ge(padded_at, 1)
            hat_products(pe, hats_b1, N_F)
        table(0)

        @on("vector")
        def _(dve):
            hat_copies(dve, hats_b1, N_F, of_vector=True)
        experts(0, x2_dram[:, :])

        @on("tensor")
        def _(pe):
            hat_products(pe, hats_b2, N_F + len(hats_b1))

        @on("scalar")
        def _(act):
            hat_copies(act, hats_b2, N_F + len(hats_b1))
        x3_done = block_b()
        attention_block(1, x3_dram, x3_done)
        table(1)
        experts(1, out[:, :, :].rearrange("s b d -> (s b) d"))

        @on("sync")
        def _(sp):
            for k in range(3):
                sp.wait_ge(stored[k], times(k, 3, 2))


        block = ctx.enter_context(nc.Block())

        @block.sync
        def _(eng):
            for stage in programs["sync"]:
                stage(eng)

        @block.gpsimd
        def _(eng):
            for stage in programs["gpsimd"]:
                stage(eng)

        @block.scalar
        def _(eng):
            for stage in programs["scalar"]:
                stage(eng)

        @block.vector
        def _(eng):
            for stage in programs["vector"]:
                stage(eng)

        @block.tensor
        def _(eng):
            for stage in programs["tensor"]:
                stage(eng)


def kernel(**inputs):
    import concourse.bacc as bacc
    from concourse.bass_utils import run_bass_kernel_spmd

    nc = bacc.Bacc("TRN2", target_bir_lowering=False, num_devices=1)
    arrays, dram = {}, {}
    for name, value in inputs.items():
        arrays[name] = np.ascontiguousarray(value)
        dram[name] = nc.dram_tensor(name, arrays[name].shape, mybir.dt.from_np(arrays[name].dtype), kind="ExternalInput").ap()
    out = nc.dram_tensor("out", (S, B, D), F32, kind="ExternalOutput").ap()
    build(nc, dram, out)
    result = run_bass_kernel_spmd(nc, [arrays], core_ids=[0])
    return result.results[0]["out"]
```
